# Optimizing a Trainium2 kernel written in Bass

```python
import numpy as np
import jax
import jax.numpy as jnp

def _softmax(x, axis=-1):
    return jax.nn.softmax(x, axis=axis)

def _gelu(x):
    return jax.nn.gelu(x, approximate=True)

def _silu(x):
    return jax.nn.silu(x)

def _sigmoid(x):
    return jax.nn.sigmoid(x)

def _layernorm(x, axis=-1, eps=1e-05):
    m = jnp.mean(x, axis=axis, keepdims=True)
    v = jnp.var(x, axis=axis, keepdims=True)
    return (x - m) / jnp.sqrt(v + eps)

def _scatter_add(tgt, idx, src, axis=0):
    return tgt.at[idx].add(src)

def _segment_sum(src, seg, n):
    return jax.ops.segment_sum(src, seg, n)
kernel_name = 'mk_conv_seq_d2_conv_nchw128_r2_a7c1d2'

def setup_inputs(seed: int=0):
    np.random.seed(seed)
    _w = jnp.asarray

    def _rec_inputs():
        import jax
        import jax.numpy as jnp
        _gk = jax.random.key(seed)
        x = -0.0005207 + 1.001 * jax.random.normal(jax.random.fold_in(_gk, 1), (4, 64, 32, 32), jnp.float32)
        return x
    x = _rec_inputs()

    def _L0_conv_setup():
        import jax, jax.numpy as jnp
        import numpy as np
        EPS = 1e-05
        GROUPS = 32

        def group_norm(x, w, b):
            B, C, H, W = x.shape
            g = x.reshape(B, GROUPS, C // GROUPS, H, W)
            mean = g.mean(axis=(2, 3, 4), keepdims=True)
            var = g.var(axis=(2, 3, 4), keepdims=True)
            g = (g - mean) * jax.lax.rsqrt(var + EPS)
            g = g.reshape(B, C, H, W)
            return g * w[None, :, None, None] + b[None, :, None, None]
        key = jax.random.key(seed)
        ks = jax.random.split(key, 8)
        B, C, H, W = (4, 64, 32, 32)
        s = 1.0 / np.sqrt(C)
        return {'x': jax.random.normal(ks[0], (B, C, H, W), jnp.float32), 'norm_w': jax.random.normal(ks[1], (C,), jnp.float32), 'norm_b': jax.random.normal(ks[2], (C,), jnp.float32), 'Wq': jax.random.normal(ks[3], (C, C), jnp.float32) * s, 'bq': jnp.zeros((C,), jnp.float32), 'Wk': jax.random.normal(ks[4], (C, C), jnp.float32) * s, 'bk': jnp.zeros((C,), jnp.float32), 'Wv': jax.random.normal(ks[5], (C, C), jnp.float32) * s, 'bv': jnp.zeros((C,), jnp.float32), 'Wo': jax.random.normal(ks[6], (C, C), jnp.float32) * s, 'bo': jnp.zeros((C,), jnp.float32)}
    _L0_conv_all = _L0_conv_setup()
    _L0_conv_in = {k: v for k, v in _L0_conv_all.items() if k in ('norm_w', 'norm_b', 'Wq', 'bq', 'Wk', 'bk', 'Wv', 'bv', 'Wo', 'bo')}
    del _L0_conv_all

    def _L1_conv_setup():
        import jax, jax.numpy as jnp
        import numpy as np
        C = 64
        NUM_GROUPS = 32
        EPS = 1e-06

        def group_norm(x, gamma, beta):
            N, Cc, H, W = x.shape
            xg = x.reshape(N, NUM_GROUPS, -1)
            mean = xg.mean(axis=-1, keepdims=True)
            var = ((xg - mean) ** 2).mean(axis=-1, keepdims=True)
            xn = ((xg - mean) * jax.lax.rsqrt(var + EPS)).reshape(N, Cc, H, W)
            return xn * gamma[None, :, None, None] + beta[None, :, None, None]

        def conv1x1(x, w, b):
            return jnp.einsum('nchw,oc->nohw', x, w) + b[None, :, None, None]
        key = jax.random.key(seed)
        ks = jax.random.split(key, 11)
        s = 1.0 / np.sqrt(C)
        return {'x': jax.random.normal(ks[0], (4, C, 32, 32), dtype=jnp.float32), 'gamma': jnp.ones((C,), jnp.float32), 'beta': jnp.zeros((C,), jnp.float32), 'wq': jax.random.normal(ks[1], (C, C), jnp.float32) * s, 'bq': jnp.zeros((C,), jnp.float32), 'wk': jax.random.normal(ks[2], (C, C), jnp.float32) * s, 'bk': jnp.zeros((C,), jnp.float32), 'wv': jax.random.normal(ks[3], (C, C), jnp.float32) * s, 'bv': jnp.zeros((C,), jnp.float32), 'wo': jax.random.normal(ks[4], (C, C), jnp.float32) * s, 'bo': jnp.zeros((C,), jnp.float32)}
    _L1_conv_all = _L1_conv_setup()
    _L1_conv_in = {k: v for k, v in _L1_conv_all.items() if k in ('gamma', 'beta', 'wq', 'bq', 'wk', 'bk', 'wv', 'bv', 'wo', 'bo')}
    del _L1_conv_all
    return {'x': x, 'L0_conv_norm_w': _L0_conv_in['norm_w'], 'L0_conv_norm_b': _L0_conv_in['norm_b'], 'L0_conv_Wq': _L0_conv_in['Wq'], 'L0_conv_bq': _L0_conv_in['bq'], 'L0_conv_Wk': _L0_conv_in['Wk'], 'L0_conv_bk': _L0_conv_in['bk'], 'L0_conv_Wv': _L0_conv_in['Wv'], 'L0_conv_bv': _L0_conv_in['bv'], 'L0_conv_Wo': _L0_conv_in['Wo'], 'L0_conv_bo': _L0_conv_in['bo'], 'L1_conv_gamma': _L1_conv_in['gamma'], 'L1_conv_beta': _L1_conv_in['beta'], 'L1_conv_wq': _L1_conv_in['wq'], 'L1_conv_bq': _L1_conv_in['bq'], 'L1_conv_wk': _L1_conv_in['wk'], 'L1_conv_bk': _L1_conv_in['bk'], 'L1_conv_wv': _L1_conv_in['wv'], 'L1_conv_bv': _L1_conv_in['bv'], 'L1_conv_wo': _L1_conv_in['wo'], 'L1_conv_bo': _L1_conv_in['bo']}

def reference(x, L0_conv_norm_w, L0_conv_norm_b, L0_conv_Wq, L0_conv_bq, L0_conv_Wk, L0_conv_bk, L0_conv_Wv, L0_conv_bv, L0_conv_Wo, L0_conv_bo, L1_conv_gamma, L1_conv_beta, L1_conv_wq, L1_conv_bq, L1_conv_wk, L1_conv_bk, L1_conv_wv, L1_conv_bv, L1_conv_wo, L1_conv_bo):
    import jax
    import jax.numpy as jnp

    def _L0_conv_ref(x, norm_w, norm_b, Wq, bq, Wk, bk, Wv, bv, Wo, bo):
        import jax, jax.numpy as jnp
        import numpy as np
        EPS = 1e-05
        GROUPS = 32

        def group_norm(x, w, b):
            B, C, H, W = x.shape
            g = x.reshape(B, GROUPS, C // GROUPS, H, W)
            mean = g.mean(axis=(2, 3, 4), keepdims=True)
            var = g.var(axis=(2, 3, 4), keepdims=True)
            g = (g - mean) * jax.lax.rsqrt(var + EPS)
            g = g.reshape(B, C, H, W)
            return g * w[None, :, None, None] + b[None, :, None, None]
        B, C, H, W = x.shape
        h = group_norm(x, norm_w, norm_b)
        h = h.transpose(0, 2, 3, 1)
        q = jnp.einsum('bhwc,cd->bhwd', h, Wq) + bq
        k = jnp.einsum('bhwc,cd->bhwd', h, Wk) + bk
        v = jnp.einsum('bhwc,cd->bhwd', h, Wv) + bv
        N = H * W
        qf = q.reshape(B, N, C)
        kf = k.reshape(B, N, C)
        vf = v.reshape(B, N, C)
        scores = jnp.einsum('bnc,bmc->bnm', qf, kf) * C ** (-0.5)
        attn = jax.nn.softmax(scores, axis=-1)
        o = jnp.einsum('bnm,bmc->bnc', attn, vf)
        o = jnp.einsum('bnc,cd->bnd', o, Wo) + bo
        o = o.reshape(B, H, W, C).transpose(0, 3, 1, 2)
        return x + o

    def _L1_conv_ref(x, gamma, beta, wq, bq, wk, bk, wv, bv, wo, bo):
        import jax, jax.numpy as jnp
        import numpy as np
        C = 64
        NUM_GROUPS = 32
        EPS = 1e-06

        def group_norm(x, gamma, beta):
            N, Cc, H, W = x.shape
            xg = x.reshape(N, NUM_GROUPS, -1)
            mean = xg.mean(axis=-1, keepdims=True)
            var = ((xg - mean) ** 2).mean(axis=-1, keepdims=True)
            xn = ((xg - mean) * jax.lax.rsqrt(var + EPS)).reshape(N, Cc, H, W)
            return xn * gamma[None, :, None, None] + beta[None, :, None, None]

        def conv1x1(x, w, b):
            return jnp.einsum('nchw,oc->nohw', x, w) + b[None, :, None, None]
        N, Cc, H, W = x.shape
        L = H * W
        xn = group_norm(x, gamma, beta)
        q = conv1x1(xn, wq, bq).reshape(N, Cc, L)
        k = conv1x1(xn, wk, bk).reshape(N, Cc, L)
        v = conv1x1(xn, wv, bv).reshape(N, Cc, L)
        scale = 1.0 / jnp.sqrt(jnp.asarray(Cc, x.dtype))
        scores = jnp.einsum('ncl,ncm->nlm', q, k) * scale
        weights = jax.nn.softmax(scores, axis=-1)
        attn = jnp.einsum('nlm,ncm->ncl', weights, v).reshape(N, Cc, H, W)
        return x + conv1x1(attn, wo, bo)

    def _gn(v, G=32, eps=1e-05):
        B_, C_, H_, W_ = v.shape
        g = v.reshape(B_, G, C_ // G, H_, W_)
        m = jnp.mean(g, axis=(2, 3, 4), keepdims=True)
        s = jnp.var(g, axis=(2, 3, 4), keepdims=True)
        return ((g - m) / jnp.sqrt(s + eps)).reshape(v.shape)

    def _ln_c(v, eps=1e-06):
        m = jnp.mean(v, axis=1, keepdims=True)
        s = jnp.var(v, axis=1, keepdims=True)
        return (v - m) / jnp.sqrt(s + eps)

    def _ln_t(v, eps=1e-05):
        m = jnp.mean(v, axis=-1, keepdims=True)
        s = jnp.var(v, axis=-1, keepdims=True)
        return (v - m) / jnp.sqrt(s + eps)

    def _to_tokens(v):
        B_, C_, H_, W_ = v.shape
        return v.reshape(B_, C_, H_ * W_).transpose(0, 2, 1)

    def _from_tokens(t, like):
        B_, C_, H_, W_ = like.shape
        return t.transpose(0, 2, 1).reshape(B_, C_, H_, W_)
    x = _L0_conv_ref(x, L0_conv_norm_w, L0_conv_norm_b, L0_conv_Wq, L0_conv_bq, L0_conv_Wk, L0_conv_bk, L0_conv_Wv, L0_conv_bv, L0_conv_Wo, L0_conv_bo)
    x = _L1_conv_ref(x, L1_conv_gamma, L1_conv_beta, L1_conv_wq, L1_conv_bq, L1_conv_wk, L1_conv_bk, L1_conv_wv, L1_conv_bv, L1_conv_wo, L1_conv_bo)
    return x

_drawn_inputs = setup_inputs


def setup_inputs(seed=0):
    import zlib

    import numpy as np

    out = dict(_drawn_inputs(seed))
    spreads = {'L0_conv_bq': (0.0, 0.389),
     'L0_conv_bk': (0.0, 0.8),
     'L0_conv_bv': (0.0, 0.1),
     'L0_conv_bo': (0.0, 0.1),
     'L1_conv_gamma': (1.0, 0.2),
     'L1_conv_beta': (0.0, 0.1),
     'L1_conv_bq': (0.0, 0.8),
     'L1_conv_bk': (0.0, 0.8),
     'L1_conv_bv': (0.0, 0.1),
     'L1_conv_bo': (0.0, 0.1)}
    factors = {}
    for name, (base, spread) in spreads.items():
        noise = np.random.default_rng([zlib.crc32(name.encode()), seed]).standard_normal(out[name].shape)
        drawn = base * np.exp(spread * noise) if base else spread * noise
        out[name] = jnp.asarray(drawn.astype(out[name].dtype))
    for name, factor in factors.items():
        out[name] = (out[name] * factor).astype(out[name].dtype)
    return out
```

```python
from contextlib import ExitStack

import concourse.bass as bass
from concourse import mybir

ALU = mybir.AluOpType
ACT = mybir.ActivationFunctionType
AX = mybir.AxisListType
F32 = mybir.dt.float32
F32R = mybir.dt.float32r

P = 128
WA, WB, WVO, NORM_W, NORM_B, BIAS_QK, EPS = 0, P, 2 * P, 3 * P, 3 * P + 1, 3 * P + 2, 3 * P + 3
UNIT_COLS = 3 * P + 4
VAL_T, OUT_W, BIAS_O, BIAS_V = UNIT_COLS, UNIT_COLS + P, UNIT_COLS + 2 * P, UNIT_COLS + 2 * P + 1
LAYER_COLS = UNIT_COLS + 2 * P + 2

LAYERS = 2
RING = 3
MAX_LEAD = 2


def attention_pair(nc, x, layer_params, consts, out):
    B, _, HALF = x.shape
    C = P // 2
    N = 2 * HALF
    TILES = N // P
    UNITS = LAYERS * B
    ADDS = TILES - 1
    SCALE = float(C) ** -0.5
    LAST_LOOP = UNITS - 2
    assert LAST_LOOP % RING == 0 and B == RING + 1

    with ExitStack() as ctx:
        def sb(name, shape, dt=F32):
            return ctx.enter_context(nc.sbuf_tensor(name, shape, dt))

        def psum(name, shape):
            return ctx.enter_context(nc.psum_tensor(name, shape, F32))

        def sem(name):
            return ctx.enter_context(nc.semaphore(name))

        xs = sb("xs", [P, ((LAYERS + 1) * B + 1) * HALF])
        layer = [sb(f"layer{n}", [P, LAYER_COLS]) for n in range(LAYERS)]
        cur = layer[0]
        const_sb = sb("const_sb", [P, 2 * P])
        ident, group_mean = const_sb[:, 0:P], const_sb[:, P:2 * P]
        ones = sb("ones", [P, C])
        started = sb("started", [P, 4])
        minus_half = sb("minus_half", [P, 1])
        out_const = sb("out_const", [P, UNITS + 1])

        stats6 = sb("stats6", [P, 6])
        means, sq_devs = stats6[:, 1::3], stats6[:, 2::3]
        mean_sum = sb("mean_sum", [P, 1])
        mean_dev = sb("mean_dev", [P, 2])
        dev_sq = sb("dev_sq", [P, 2])
        var_about = sb("var_about", [P, 2])
        var_eps = sb("var_eps", [P, 1])
        rstd = sb("rstd", [P, 1])
        gain = sb("gain", [P, 1])
        neg_shift = sb("neg_shift", [P, 1])
        h = sb("h", [P, HALF])
        qk_hi = sb("qk_hi", [P, N], F32R)
        qk_lo = sb("qk_lo", [P, N], F32R)
        q_both = [sb(f"q_both{b}", [P, N], F32R) for b in range(RING)]
        k_twice = [sb(f"k_twice{b}", [P, N], F32R) for b in range(RING)]
        q_max = [sb(f"q_max{b}", [P, N], F32R) for b in range(RING)]
        k_low = [sb(f"k_low{b}", [P, N], F32R) for b in range(RING)]
        vals = [sb(f"vals{b}", [P, HALF]) for b in range(RING)]
        neg_max = [sb(f"neg_max{b}", [P, TILES]) for b in range(RING)]
        max_rows = sb("max_rows", [TILES, P], F32R)
        probs = [sb(f"probs{t}", [P, N]) for t in range(TILES)]
        prob_sum = [sb(f"prob_sum{b}", [P, N]) for b in range(RING)]
        attn = sb("attn", [P, HALF])
        rden = sb("rden", [P, HALF])
        scaled = sb("scaled", [P, HALF])

        ps_scores = [psum(f"ps_scores{b}", [P, N]) for b in range(2)]
        ps_max = psum("ps_max", [P, N])
        ps_attn = psum("ps_attn", [P, HALF])
        ps_misc = psum("ps_misc", [P, HALF])

        x_in = [sem(f"x_in{b}") for b in range(B)]
        params_in = [sem(f"params_in{n}") for n in range(LAYERS)]
        consts_in = sem("consts_in")
        filled = sem("filled")
        setup_mm = sem("setup_mm")
        setup_done = sem("setup_done")
        gn_step = sem("gn_step")
        group_stat = sem("group_stat")
        var_ready = sem("var_ready")
        rstd_ready = sem("rstd_ready")
        h_ready = sem("h_ready")
        qk_ready = sem("qk_ready")
        hi_done = sem("hi_done")
        lo_done = sem("lo_done")
        spread = [sem(f"spread{b}") for b in range(RING)]
        v_ready = sem("v_ready")
        v_copied = sem("v_copied")
        max_mm = sem("max_mm")
        max_done = sem("max_done")
        max_turned = sem("max_turned")
        max_staged = sem("max_staged")
        max_in = [sem(f"max_in{b}") for b in range(RING)]
        scores_ready = sem("scores_ready")
        exp_done = sem("exp_done")
        probs_read = sem("probs_read")
        probs_added = sem("probs_added")
        attn_copied = sem("attn_copied")
        den_ready = sem("den_ready")
        rden_done = sem("rden_done")
        scaled_done = sem("scaled_done")
        final_done = sem("final_done")
        stored = sem("stored")
        low_zero = sem("low_zero")
        layer_switched = sem("layer_switched")

        GN = 8
        SPREADS = 12

        def slot(unit):
            return bass.ds((unit + 1) * HALF, HALF)

        def halves():
            return (slice(0, HALF), slice(HALF, N))

        block = ctx.enter_context(nc.Block())

        def in_ring(r, i, d):
            return (r + d) % RING, i + (r + d) // RING

        @block.sync
        def _(sp):
            for half in range(2):
                rows = slice(half * C, half * C + C)
                sp.dma_start(xs[rows, HALF:2 * HALF], x[0, rows, :]).then_inc(x_in[0], 16)
            sp.dma_start(const_sb[:, :], consts).then_inc(consts_in, 16)
            for b in range(1, B):
                sp.dma_start(xs[:, (b + 1) * HALF:(b + 2) * HALF], x[b]).then_inc(x_in[b], 16)

            def spread_qk(unit, b, unit_before_done):
                if unit_before_done is not None:
                    sp.wait_ge(scores_ready, unit_before_done)
                for half, cols in enumerate(halves()):
                    sp.wait_ge(hi_done, 2 * unit + half + 1)
                    moves = [(q_both[b][0:C, cols], qk_hi[0:C, cols]), (q_max[b][0:C, cols], qk_hi[0:C, cols]),
                             (k_twice[b][0:C, cols], qk_hi[C:P, cols]), (k_twice[b][C:P, cols], qk_hi[C:P, cols]),
                             (q_both[b][C:P, cols], qk_lo[0:C, cols]), (k_low[b][0:C, cols], qk_lo[C:P, cols])]
                    for n, (dst, src) in enumerate(moves):
                        if n == 4:
                            sp.wait_ge(lo_done, 2 * unit + half + 1)
                        sp.dma_start(dst.bitcast(F32), src.bitcast(F32)).then_inc(spread[b], 16)

            def place_max(unit, b):
                sp.wait_ge(max_staged, unit + 1)
                row = q_max[b][C:C + 1, :].bitcast(F32).rearrange("p (t n) -> p t n", t=TILES)
                sp.dma_start(row, max_rows[:, :].bitcast(F32)).then_inc(max_in[b], 16)

            def window(w, r, prep, nxt):
                if prep:
                    spread_qk(w + 2, (r + 2) % RING, TILES * w + 1)
                if nxt:
                    place_max(w + 1, (r + 1) % RING)

            sp.wait_ge(filled, RING)
            spread_qk(0, 0, None)
            spread_qk(1, 1, None)
            place_max(0, 0)
            with sp.Fori(0, LAST_LOOP // RING) as i:
                for r in range(RING):
                    window(i * RING + r, r, True, True)
            window(UNITS - 2, 0, False, True)
            for image in range(B):
                unit = UNITS - B + image
                sp.wait_ge(final_done, unit + 2)
                s = (unit + B + 1) * HALF
                sp.dma_start(out[image], xs[:, s:s + HALF]).then_inc(stored, 16)
            sp.wait_ge(stored, 16 * B)

        @block.gpsimd
        def _(pool):
            pool.memset(ones[:, :], 1.0).then_inc(probs_added, ADDS)
            pool.wait_ge(probs_added, ADDS)
            pool.memset(minus_half[:, :], -0.5).then_inc(probs_read, TILES)
            pool.wait_ge(probs_read, TILES)

            def root(unit):
                pool.wait_ge(var_ready, unit + 1)
                pool.tensor_tensor(rstd[:, :], var_eps[:, :], minus_half[:, :], ALU.pow).then_inc(rstd_ready, 1)

            def add(w, b, t):
                pool.wait_ge(exp_done, TILES * w + t + 2)
                first = probs[0] if t == 1 else prob_sum[b]
                pool.wait_ge(probs_added, ADDS * (w + 1) + t - 1)
                pool.tensor_tensor(prob_sum[b][:, :], first[:, :], probs[t][:, :], ALU.add).then_inc(probs_added, 1)

            def window(w, r, prep):
                for t in range(1, TILES):
                    add(w, r, t)
                    if t == 1 and prep:
                        root(w + 2)

            root(0)
            root(1)
            with pool.Fori(0, LAST_LOOP // RING) as i:
                for r in range(RING):
                    window(i * RING + r, r, True)
            for w in range(LAST_LOOP, UNITS):
                window(w, w % RING, False)

        @block.scalar
        def _(act):
            for n in range(LAYERS):
                act.dma_start(layer[n][:, :], layer_params[n]).then_inc(params_in[n], 16)

            def qk_high(unit, half, before):
                if half == 0 and before:
                    act.wait_ge(spread[before[0]], 16 * SPREADS * (before[1] + 1))
                act.wait_ge(qk_ready, 2 * unit + half + 1)
                act.activation(qk_hi[:, halves()[half]], ps_misc[:, :], ACT.Identity,
                               bias=cur[:, BIAS_QK:BIAS_QK + 1]).then_inc(hi_done, 1)

            def copy_v(unit, b):
                act.wait_ge(v_ready, unit + 1)
                act.activation(vals[b][:, :], ps_misc[:, :], ACT.Copy).then_inc(v_copied, 1)

            def stage_max(unit, before):
                if before:
                    act.wait_ge(max_in[before[0]], 16 * (before[1] + 1))
                act.wait_ge(max_turned, unit + 1)
                act.activation(max_rows[:, :], ps_misc[0:TILES, 0:P], ACT.Copy).then_inc(max_staged, 1)

            def exp(unit, t):
                act.wait_ge(scores_ready, TILES * unit + t + 1)
                act.wait_ge(probs_read, TILES * unit + t + 1)
                act.wait_ge(probs_added, ADDS * unit + max(t, 1))
                act.activation(probs[t][:, :], ps_scores[t % 2][:, :], ACT.Exp, scale=SCALE).then_inc(exp_done, 1)

            def copy_attn(unit):
                act.wait_ge(probs_read, TILES * (unit + 2))
                act.wait_ge(final_done, unit + 1)
                act.activation(attn[:, :], ps_attn[:, :], ACT.Copy).then_inc(attn_copied, 1)

            def window(w, r, i, prep, nxt, more):
                for t in range(TILES):
                    if t + 1 < TILES:
                        exp(w, t + 1)
                    elif more:
                        exp(w + 1, 0)
                    if prep and t == 2:
                        qk_high(w + 2, 0, in_ring(r, i, 1))
                    if prep and t == 3:
                        qk_high(w + 2, 1, None)
                    if prep and t == 4:
                        copy_v(w + 2, (r + 2) % RING)
                    if nxt and t == 6:
                        stage_max(w + 1, in_ring(r, i, 0))
                copy_attn(w)

            for u in range(2):
                qk_high(u, 0, (0, 0) if u else None)
                qk_high(u, 1, None)
                copy_v(u, u)
            stage_max(0, None)
            exp(0, 0)
            with act.Fori(0, LAST_LOOP // RING) as i:
                for r in range(RING):
                    window(i * RING + r, r, i, True, True, True)
            for w in range(LAST_LOOP, UNITS):
                window(w, w % RING, w // RING, False, w + 1 < UNITS, w + 1 < UNITS)

        @block.vector
        def _(dve):

            def gn_stats(unit):
                dve.bn_stats(stats6[:, :], xs[:, slot(unit)]).then_inc(gn_step, 1)
                dve.wait_ge(gn_step, GN * unit + 1)
                dve.tensor_tensor(mean_sum[:, :], means[:, 0:1], means[:, 1:2], ALU.add).then_inc(gn_step, 1)

            def gn_about(unit):
                dve.wait_ge(group_stat, 2 * unit + 1)
                dve.tensor_scalar(mean_dev[:, :], means, ps_misc[:, 0:1], None, ALU.subtract).then_inc(gn_step, 1)
                dve.wait_ge(gn_step, GN * unit + 3)
                dve.tensor_tensor(dev_sq[:, :], mean_dev[:, :], mean_dev[:, :], ALU.mult).then_inc(gn_step, 1)
                dve.wait_ge(gn_step, GN * unit + 4)
                dve.scalar_tensor_tensor(out=var_about[:, :], in0=sq_devs, scalar=2.0 / HALF, in1=dev_sq[:, :],
                                         op0=ALU.mult, op1=ALU.add).then_inc(gn_step, 1)

            def gn_var(unit):
                dve.wait_ge(group_stat, 2 * unit + 2)
                dve.tensor_scalar(var_eps[:, :], ps_misc[:, 1:2], cur[:, EPS:EPS + 1], None, ALU.add).then_inc(var_ready, 1)

            def gn_apply(unit):
                dve.wait_ge(rstd_ready, unit + 1)
                dve.tensor_tensor(gain[:, :], rstd[:, :], cur[:, NORM_W:NORM_W + 1], ALU.mult).then_inc(gn_step, 1)
                dve.wait_ge(gn_step, GN * unit + 6)
                dve.scalar_tensor_tensor(out=neg_shift[:, :], in0=ps_misc[:, 0:1], scalar=gain[:, :],
                                         in1=cur[:, NORM_B:NORM_B + 1], op0=ALU.mult, op1=ALU.subtract).then_inc(gn_step, 1)
                dve.wait_ge(gn_step, GN * unit + 7)
                dve.wait_ge(v_copied, unit)
                dve.tensor_scalar(h[:, :], xs[:, slot(unit)], gain[:, :], neg_shift[:, :],
                                  ALU.mult, ALU.subtract).then_inc(gn_step, 1)

            def qk_low(unit, half):
                cols = halves()[half]
                dve.wait_ge(hi_done, 2 * unit + half + 1)
                dve.scalar_tensor_tensor(out=qk_lo[:, cols], in0=ps_misc[:, :], scalar=cur[:, BIAS_QK:BIAS_QK + 1],
                                         in1=qk_hi[:, cols].bitcast(F32), op0=ALU.add,
                                         op1=ALU.subtract).then_inc(lo_done, 1)

            def row_max(unit, b, t):
                dve.wait_ge(max_mm, TILES * unit + t + 1)
                dve.tensor_reduce(neg_max[b][:, t:t + 1], ps_max[:, :], AX.X, ALU.max, negate=True).then_inc(max_done, 1)

            def reciprocal(unit):
                dve.wait_ge(den_ready, unit + 1)
                dve.reciprocal(rden[:, :], ps_misc[:, :]).then_inc(rden_done, 1)

            def final(unit):
                dve.wait_ge(attn_copied, unit + 2)
                dve.wait_ge(rden_done, unit + 2)
                dve.tensor_tensor(scaled[:, :], attn[:, :], rden[:, :], ALU.mult).then_inc(scaled_done, 1)
                dve.wait_ge(scaled_done, unit + 1)
                dve.scalar_tensor_tensor(out=xs[:, slot(unit + B)], in0=scaled[:, :], scalar=out_const[:, bass.ds(unit + 1, 1)],
                                         in1=xs[:, slot(unit)], op0=ALU.add, op1=ALU.add).then_inc(final_done, 1)

            def window(w, r, i, prep, nxt, last):
                if prep and r == RING - 1:
                    dve.wait_ge(v_copied, w + 2)
                    dve.wait_ge(setup_done, 2 * LAYERS)
                    dve.tensor_copy(cur[:, 0:UNIT_COLS], layer[1][:, 0:UNIT_COLS]).then_inc(layer_switched, 1)
                for t in range(TILES):
                    if prep and t == 0:
                        gn_stats(w + 2)
                    if prep and t == 1:
                        if r == RING - 1:
                            dve.wait_ge(layer_switched, i + 1)
                        gn_about(w + 2)
                        gn_var(w + 2)
                    if prep and t == 2:
                        gn_apply(w + 2)
                    if prep and t == 3:
                        qk_low(w + 2, 0)
                    if prep and t == 4:
                        qk_low(w + 2, 1)
                    if t == 5:
                        if isinstance(w, int):
                            last(w)
                        elif r == 0:
                            with dve.If(i > 0):
                                last(w)
                        else:
                            last(w)
                        dve.wait_ge(final_done, w + 1)
                    m = t + MAX_LEAD
                    if m < TILES and nxt:
                        row_max(w + 1, (r + 1) % RING, m)
                    elif m >= TILES and prep:
                        row_max(w + 2, (r + 2) % RING, m - TILES)

            def finish(w):
                reciprocal(w - 1)
                final(w - 1)

            def setup(n):
                dve.wait_ge(setup_mm, n + 1)
                dve.wait_ge(params_in[n], 16)
                for half in range(2):
                    rows = slice(half * C, half * C + C)
                    dve.tensor_copy(layer[n][rows, WVO + half * C:WVO + half * C + C], ps_misc[rows, 0:C])
                dve.tensor_scalar(out_const[:, n * B + 1:(n + 1) * B + 1], ones[:, 0:B], ps_misc[:, C:C + 1],
                                  layer[n][:, BIAS_O:BIAS_O + 1], ALU.mult, ALU.add).then_inc(setup_done, 1)
                dve.memset(layer[n][:, EPS:EPS + 1], (1e-5, 1e-6)[n]).then_inc(setup_done, 1)

            for n, start_at_1 in enumerate((exp_done, attn_copied, rden_done, final_done)):
                dve.memset(started[:, n:n + 1], 0.0).then_inc(start_at_1, 1)
            for b in range(RING):
                dve.memset(k_low[b][C:P, :].bitcast(F32), 0.0).then_inc(low_zero, 1)
                dve.memset(q_max[b][C:P, :].bitcast(F32), 0.0).then_inc(low_zero, 1)
            dve.wait_ge(low_zero, 2 * RING)
            for b in range(RING):
                dve.memset(k_low[b][C:C + 1, :].bitcast(F32), 1.0).then_inc(filled, 1)
            dve.wait_ge(probs_added, ADDS)
            setup(0)
            for u in range(2):
                dve.wait_ge(x_in[u], 32 if u == 0 else 16)
                dve.wait_ge(setup_done, 2)
                gn_stats(u)
                gn_about(u)
                gn_var(u)
                gn_apply(u)
                qk_low(u, 0)
                qk_low(u, 1)
            setup(1)
            for t in range(TILES):
                row_max(0, 0, t)
            for t in range(MAX_LEAD):
                row_max(1, 1, t)
            for b in range(2, B):
                dve.wait_ge(x_in[b], 16)
            with dve.Fori(0, LAST_LOOP // RING) as i:
                for r in range(RING):
                    window(i * RING + r, r, i, True, True, finish)
            for w in range(LAST_LOOP, UNITS):
                window(w, w % RING, w // RING, False, w + 1 < UNITS, finish)
            finish(UNITS)

        @block.tensor
        def _(pe):
            def group_mean_of(unit):
                pe.wait_ge(gn_step, GN * unit + 2)
                pe.matmul(ps_misc[:, 0:1], group_mean, mean_sum[:, :], start=True, stop=True).then_inc(group_stat, 1)

            def group_var_of(unit):
                pe.wait_ge(gn_step, GN * unit + 5)
                for parity in range(2):
                    mm = pe.matmul(ps_misc[:, 1:2], group_mean, var_about[:, parity:parity + 1],
                                   start=(parity == 0), stop=(parity == 1))
                mm.then_inc(group_stat, 1)

            def project_qk(unit, half):
                if half == 0:
                    pe.wait_ge(gn_step, GN * unit + 8)
                else:
                    pe.wait_ge(lo_done, 2 * unit + 1)
                w = cur[:, (WA, WB)[half]:(WA, WB)[half] + P]
                pe.matmul(ps_misc[:, :], w, h[:, :], start=True, stop=True).then_inc(qk_ready, 1)

            def project_v(unit):
                pe.wait_ge(lo_done, 2 * unit + 2)
                for j in range(HALF // P):
                    cols = slice(j * P, (j + 1) * P)
                    mm = pe.matmul(ps_misc[:, cols], h[:, cols], cur[:, WVO:WVO + P], start=True, stop=True)
                mm.then_inc(v_ready, 1)

            def max_scores(unit, b, rounds, t):
                if t == 0:
                    pe.wait_ge(spread[b], 16 * SPREADS * (rounds + 1))
                pe.wait_ge(max_done, TILES * unit + t)
                for cols in halves():
                    mm = pe.matmul(ps_max[:, cols], q_both[b][:, t * P:(t + 1) * P], k_twice[b][:, cols],
                                   start=True, stop=True)
                mm.then_inc(max_mm, 1)

            def turn_max(unit, b):
                pe.wait_ge(max_done, TILES * (unit + 1))
                pe.transpose(ps_misc[0:TILES, 0:P], neg_max[b][:, :], ident).then_inc(max_turned, 1)

            def scores(unit, b, rounds, t):
                if t == 0:
                    pe.wait_ge(spread[b], 16 * SPREADS * (rounds + 1))
                    pe.wait_ge(max_in[b], 16 * (rounds + 1))
                if not (isinstance(unit, int) and unit == 0 and t < 2):
                    pe.wait_ge(exp_done, TILES * unit + t)
                keys = slice(t * P, (t + 1) * P)
                ps = ps_scores[t % 2]
                for cols in halves():
                    pe.matmul(ps[:, cols], k_twice[b][:, keys], q_both[b][:, cols], start=True, stop=False)
                for cols in halves():
                    mm = pe.matmul(ps[:, cols], k_low[b][:, keys], q_max[b][:, cols], start=False, stop=True)
                mm.then_inc(scores_ready, 1)

            def values(unit, b, t):
                if t == 0:
                    pe.wait_ge(v_copied, unit + 1)
                    pe.wait_ge(attn_copied, unit + 1)
                pe.wait_ge(exp_done, TILES * unit + t + 2)
                half, j = divmod(t, TILES // 2)
                v = vals[b][:, j * P + half * C:j * P + half * C + C]
                for n, cols in enumerate(halves()):
                    mm = pe.matmul(ps_attn[n * C:(n + 1) * C, :], v, probs[t][:, cols],
                                   start=(t == 0), stop=(t == TILES - 1))
                mm.then_inc(probs_read, 1)

            def denominators(unit, b):
                pe.wait_ge(probs_added, ADDS * (unit + 2))
                for n, cols in enumerate(halves()):
                    mm = pe.matmul(ps_misc[n * C:(n + 1) * C, :], ones[:, :], prob_sum[b][:, cols],
                                   start=True, stop=True)
                mm.then_inc(den_ready, 1)

            def window(w, r, i, prep, nxt):
                for t in range(TILES):
                    if t + 1 < TILES:
                        scores(w, *in_ring(r, i, 0), t + 1)
                    elif nxt:
                        scores(w + 1, *in_ring(r, i, 1), 0)
                    if prep and t == 0:
                        pe.wait_ge(max_staged, w + 1)
                        group_mean_of(w + 2)
                    m = t + MAX_LEAD
                    if m < TILES and nxt:
                        max_scores(w + 1, *in_ring(r, i, 1), m)
                    elif m >= TILES and prep:
                        max_scores(w + 2, *in_ring(r, i, 2), m - TILES)
                    if prep and t == 1:
                        group_var_of(w + 2)
                    if prep and t == 2:
                        project_qk(w + 2, 0)
                    if prep and t == 3:
                        project_qk(w + 2, 1)
                    if prep and t == 4:
                        project_v(w + 2)
                    values(w, r, t)
                    if t == 4:
                        if isinstance(w, int):
                            pe.wait_ge(v_copied, min(w + 3, UNITS))
                            denominators(w - 1, (r - 1) % RING)
                        elif r == 0:
                            with pe.If(i > 0):
                                pe.wait_ge(v_copied, w + 3)
                                denominators(w - 1, (r - 1) % RING)
                        else:
                            pe.wait_ge(v_copied, w + 3)
                            denominators(w - 1, (r - 1) % RING)
                    if nxt and t == 6:
                        pe.wait_ge(rden_done, w + 1)
                        if r == 0 and not isinstance(w, int):
                            pe.wait_ge(v_copied, w + 3)
                        turn_max(w + 1, (r + 1) % RING)

            def setup(n):
                p = layer[n]
                pe.wait_ge(params_in[n], 16)
                pe.matmul(ps_misc[:, 0:C], p[0:C, VAL_T:VAL_T + P], p[0:C, OUT_W:OUT_W + C], start=True, stop=True)
                pe.matmul(ps_misc[:, C:C + 1], p[0:C, OUT_W:OUT_W + P], p[0:C, BIAS_V:BIAS_V + 1],
                          start=True, stop=True).then_inc(setup_mm, 1)

            pe.wait_ge(consts_in, 16)
            setup(0)
            for u in range(2):
                pe.wait_ge(setup_done, 2)
                if u:
                    pe.wait_ge(v_copied, u)
                group_mean_of(u)
                group_var_of(u)
                project_qk(u, 0)
                project_qk(u, 1)
                project_v(u)
            pe.wait_ge(v_copied, 2)
            setup(1)
            for t in range(TILES):
                max_scores(0, 0, 0, t)
            pe.wait_ge(setup_done, 4)
            turn_max(0, 0)
            for t in range(MAX_LEAD):
                max_scores(1, 1, 0, t)
            scores(0, 0, 0, 0)
            with pe.Fori(0, LAST_LOOP // RING) as i:
                for r in range(RING):
                    window(i * RING + r, r, i, True, True)
            for w in range(LAST_LOOP, UNITS):
                window(w, w % RING, w // RING, False, w + 1 < UNITS)
            pe.wait_ge(rden_done, UNITS)
            denominators(UNITS - 1, (UNITS - 1) % RING)



def pack_layer(np, wq, wk, bq, bk, v_rows, o_cols, bv, bo, norm_w, norm_b):
    C = wq.shape[0]
    p = np.zeros((P, LAYER_COLS), wq.dtype)
    for half, at in enumerate((WA, WB)):
        rows = slice(half * C, half * C + C)
        p[rows, at:at + C] = wq
        p[rows, at + C:at + P] = wk
        p[rows, NORM_W] = norm_w
        p[rows, NORM_B] = norm_b
        p[rows, BIAS_QK] = (bq, bk)[half]
        p[rows, BIAS_O] = bo
        p[0:C, VAL_T + half * C:VAL_T + half * C + C] = v_rows
        p[0:C, OUT_W + half * C:OUT_W + half * C + C] = o_cols
    p[0:C, BIAS_V] = bv
    return p


def kernel(**inputs):
    import numpy as np
    import concourse.bacc as bacc
    from concourse.bass_utils import run_bass_kernel_spmd

    a = {k: np.asarray(v) for k, v in inputs.items()}
    x = a["x"]
    B, C, H, W = x.shape
    half = H * W // 2
    xh = np.ascontiguousarray(x.reshape(B, C, 2, half).transpose(0, 2, 1, 3).reshape(B, 2 * C, half))
    g0 = lambda n: a["L0_conv_" + n]
    g1 = lambda n: a["L1_conv_" + n]
    layers = np.stack([
        pack_layer(np, g0("Wq"), g0("Wk"), g0("bq"), g0("bk"), g0("Wv").T, g0("Wo"), g0("bv"), g0("bo"),
                   g0("norm_w"), g0("norm_b")),
        pack_layer(np, g1("wq").T, g1("wk").T, g1("bq"), g1("bk"), g1("wv"), g1("wo").T, g1("bv"), g1("bo"),
                   g1("gamma"), g1("beta")),
    ])
    per_group = C // 32
    group = np.arange(P) % C // per_group
    consts = np.concatenate([np.eye(P), (group[:, None] == group[None, :]) / (4 * per_group)], 1).astype(np.float32)

    nc = bacc.Bacc("TRN2", target_bir_lowering=False, num_devices=1)
    arrays = {"x_dram": xh, "layers_dram": layers, "consts_dram": consts}
    aps = [nc.dram_tensor(k, v.shape, F32, kind="ExternalInput").ap() for k, v in arrays.items()]
    out = nc.dram_tensor("out_dram", xh.shape, F32, kind="ExternalOutput").ap()
    attention_pair(nc, *aps, out)
    r = run_bass_kernel_spmd(nc, [arrays], core_ids=[0])
    got = r.results[0]["out_dram"]
    return got.reshape(B, 2, C, half).transpose(0, 2, 1, 3).reshape(B, C, H, W)
```

```python
from contextlib import ExitStack

import concourse.bass as bass
from concourse import mybir

ALU = mybir.AluOpType
ACT = mybir.ActivationFunctionType
AX = mybir.AxisListType
F32 = mybir.dt.float32
F32R = mybir.dt.float32r

P = 128
WA, WB, WVO, NORM_W, NORM_B, BIAS_QK, EPS = 0, P, 2 * P, 3 * P, 3 * P + 1, 3 * P + 2, 3 * P + 3
UNIT_COLS = 3 * P + 4
VAL_T, OUT_W, BIAS_O, BIAS_V = UNIT_COLS, UNIT_COLS + P, UNIT_COLS + 2 * P, UNIT_COLS + 2 * P + 1
LAYER_COLS = UNIT_COLS + 2 * P + 2

LAYERS = 2
RING = 3
MAX_LEAD = 3


def attention_pair(nc, x, layer_params, consts, out):
    B, _, HALF = x.shape
    C = P // 2
    N = 2 * HALF
    TILES = N // P
    UNITS = LAYERS * B
    ADDS = TILES - 1
    SCALE = float(C) ** -0.5
    LAST_LOOP = UNITS - 2
    assert LAST_LOOP % RING == 0 and B == RING + 1

    with ExitStack() as ctx:
        def sb(name, shape, dt=F32):
            return ctx.enter_context(nc.sbuf_tensor(name, shape, dt))

        def psum(name, shape):
            return ctx.enter_context(nc.psum_tensor(name, shape, F32))

        def sem(name):
            return ctx.enter_context(nc.semaphore(name))

        xs = sb("xs", [P, ((LAYERS + 1) * B + 1) * HALF])
        layer = [sb(f"layer{n}", [P, LAYER_COLS]) for n in range(LAYERS)]
        cur = layer[0]
        const_sb = sb("const_sb", [P, 2 * P])
        ident, group_mean = const_sb[:, 0:P], const_sb[:, P:2 * P]
        ones = sb("ones", [P, C])
        started = sb("started", [P, 6])
        minus_half = sb("minus_half", [P, 1])
        out_const = sb("out_const", [P, UNITS + 1])

        stats6 = sb("stats6", [P, 6])
        means, sq_devs = stats6[:, 1::3], stats6[:, 2::3]
        mean = sb("mean", [P, 1])
        mean_dev = sb("mean_dev", [P, 2])
        dev_sq = sb("dev_sq", [P, 2])
        var_about = sb("var_about", [P, 2])
        var_eps = sb("var_eps", [P, 1])
        rstd = sb("rstd", [P, 1])
        gain = sb("gain", [P, 1])
        neg_shift = sb("neg_shift", [P, 1])
        h = sb("h", [P, HALF])
        qk_hi = sb("qk_hi", [P, N], F32R)
        qk_lo = sb("qk_lo", [P, N], F32R)
        q_sides = [sb(f"q_sides{b}", [P, 2, N], F32R) for b in range(RING)]
        q_both = [q_sides[b][:, 0] for b in range(RING)]
        q_max = [q_sides[b][:, 1] for b in range(RING)]
        k_twice = [sb(f"k_twice{b}", [P, N], F32R) for b in range(RING)]
        k_low = [sb(f"k_low{b}", [P, N], F32R) for b in range(RING)]
        vals = [sb(f"vals{b}", [P, HALF]) for b in range(RING)]
        neg_max = [sb(f"neg_max{b}", [P, TILES]) for b in range(RING)]
        max_rows = sb("max_rows", [TILES, P], F32R)
        probs = [sb(f"probs{t}", [P, N]) for t in range(TILES)]
        prob_sum = [sb(f"prob_sum{b}", [P, N]) for b in range(RING)]
        attn = [sb(f"attn{b}", [P, HALF]) for b in range(RING)]
        den = sb("den", [P, HALF])
        rden = sb("rden", [P, HALF])
        scaled = sb("scaled", [P, HALF])

        ps_scores = [psum(f"ps_scores{b}", [P, N]) for b in range(2)]
        ps_max = psum("ps_max", [P, N])
        ps_attn = psum("ps_attn", [P, HALF])
        ps_misc = psum("ps_misc", [P, HALF])

        x_in = [sem(f"x_in{b}") for b in range(B)]
        params_in = [sem(f"params_in{n}") for n in range(LAYERS)]
        consts_in = sem("consts_in")
        rows_filled = sem("rows_filled")
        setup_mm = sem("setup_mm")
        setup_done = sem("setup_done")
        gn_step = sem("gn_step")
        group_stat = sem("group_stat")
        var_ready = sem("var_ready")
        rstd_ready = sem("rstd_ready")
        h_ready = sem("h_ready")
        qk_ready = sem("qk_ready")
        hi_done = sem("hi_done")
        k_placed = sem("k_placed")
        lo_done = sem("lo_done")
        spread = [sem(f"spread{b}") for b in range(RING)]
        v_ready = sem("v_ready")
        v_copied = sem("v_copied")
        max_mm = sem("max_mm")
        max_done = sem("max_done")
        max_turned = sem("max_turned")
        max_staged = sem("max_staged")
        max_in = [sem(f"max_in{b}") for b in range(RING)]
        scores_ready = sem("scores_ready")
        exp_done = sem("exp_done")
        probs_read = sem("probs_read")
        probs_added = sem("probs_added")
        attn_copied = sem("attn_copied")
        den_ready = sem("den_ready")
        den_copied = sem("den_copied")
        rden_done = sem("rden_done")
        scaled_done = sem("scaled_done")
        final_done = sem("final_done")
        stored = sem("stored")
        layer_switched = sem("layer_switched")

        CHUNKS = 4
        GN = 8
        SPREADS = 6

        def slot(unit):
            return bass.ds((unit + 1) * HALF, HALF)

        def slot_part(unit, part):
            return bass.ds((unit + 1) * HALF + part * (HALF // 2), HALF // 2)

        FIRST_MAX = (ps_scores[0], ps_scores[1], ps_max)

        def halves():
            return (slice(0, HALF), slice(HALF, N))

        block = ctx.enter_context(nc.Block())

        def in_ring(r, i, d):
            return (r + d) % RING, i + (r + d) // RING

        @block.sync
        def _(sp):
            for b in range(B):
                if b == 1:
                    sp.dma_start(const_sb[:, :], consts).then_inc(consts_in, 16)
                sp.dma_start(xs[:, (b + 1) * HALF:(b + 2) * HALF], x[b]).then_inc(x_in[b], 16)

            def spread_qk(unit, b, unit_before_done):
                if unit_before_done is not None:
                    sp.wait_ge(scores_ready, unit_before_done)
                for half, cols in enumerate(halves()):
                    q_hi = qk_hi[0:C, cols].bitcast(F32)
                    q_lo, k_lo = (qk_lo[rows, cols].bitcast(F32) for rows in (slice(0, C), slice(C, P)))
                    sp.wait_ge(hi_done, 2 * unit + half + 1)
                    sp.dma_start(q_sides[b][0:C, :, cols].bitcast(F32),
                                 q_hi.unsqueeze(1).broadcast_to([C, 2, HALF])).then_inc(spread[b], 16)
                    sp.wait_ge(lo_done, 2 * unit + half + 1)
                    sp.dma_start(q_both[b][C:P, cols].bitcast(F32), q_lo).then_inc(spread[b], 16)
                    sp.dma_start(k_low[b][0:C, cols].bitcast(F32), k_lo).then_inc(spread[b], 16)

            def place_max(unit, b):
                sp.wait_ge(max_staged, unit + 1)
                row = q_max[b][C:C + 1, :].bitcast(F32).rearrange("p (t n) -> p t n", t=TILES)
                sp.dma_start(row, max_rows[:, :].bitcast(F32)).then_inc(max_in[b], 16)

            def window(w, r, prep, nxt):
                if prep:
                    spread_qk(w + 2, (r + 2) % RING, TILES * w + 1)
                if nxt:
                    place_max(w + 1, (r + 1) % RING)

            spread_qk(0, 0, None)
            spread_qk(1, 1, None)
            place_max(0, 0)
            with sp.Fori(0, LAST_LOOP // RING) as i:
                for r in range(RING):
                    window(i * RING + r, r, True, True)
            window(UNITS - 2, 0, False, True)
            for image in range(B):
                unit = UNITS - B + image
                parts = 1 if unit < UNITS - 1 else CHUNKS
                for part in range(parts):
                    sp.wait_ge(final_done, 2 * (unit + 1) + 1 if parts == 1 else 2 * unit + part + 2)
                    cols = slice(part * HALF // parts, (part + 1) * HALF // parts)
                    src = xs[:, (unit + B + 1) * HALF + cols.start:(unit + B + 1) * HALF + cols.stop]
                    sp.dma_start(out[image, :, cols], src).then_inc(stored, 16)
            sp.wait_ge(stored, 16 * (B - 1 + CHUNKS))

        @block.gpsimd
        def _(pool):
            pool.memset(ones[:, :], 1.0).then_inc(probs_added, ADDS)
            pool.wait_ge(probs_added, ADDS)
            pool.memset(minus_half[:, :], -0.5).then_inc(probs_read, TILES)
            pool.wait_ge(probs_read, TILES)

            def root(unit):
                pool.wait_ge(var_ready, unit + 1)
                pool.tensor_tensor(rstd[:, :], var_eps[:, :], minus_half[:, :], ALU.pow).then_inc(rstd_ready, 1)

            def add(w, b, t):
                pool.wait_ge(exp_done, TILES * w + t + 2)
                first = probs[0] if t == 1 else prob_sum[b]
                pool.wait_ge(probs_added, ADDS * (w + 1) + t - 1)
                pool.tensor_tensor(prob_sum[b][:, :], first[:, :], probs[t][:, :], ALU.add).then_inc(probs_added, 1)

            def window(w, r, prep):
                for t in range(1, TILES):
                    add(w, r, t)
                    if t == 1 and prep:
                        root(w + 2)

            root(0)
            for b in range(RING):
                if b:
                    pool.wait_ge(rows_filled, 2 * b)
                else:
                    pool.wait_ge(rstd_ready, 1)
                pool.memset(k_low[b][C:P, :].bitcast(F32), 0.0).then_inc(rows_filled, 1)
                pool.wait_ge(rows_filled, 2 * b + 1)
                pool.memset(q_max[b][C:P, :].bitcast(F32), 0.0).then_inc(rows_filled, 1)
            pool.wait_ge(rows_filled, 2 * RING)
            root(1)
            pool.wait_ge(rstd_ready, 2)
            for b in range(RING):
                pool.memset(k_low[b][C:C + 1, :].bitcast(F32), 1.0).then_inc(rows_filled, 1)
            pool.wait_ge(rows_filled, 3 * RING)
            with pool.Fori(0, LAST_LOOP // RING) as i:
                for r in range(RING):
                    window(i * RING + r, r, True)
            window(UNITS - 2, (UNITS - 2) % RING, False)

        @block.scalar
        def _(act):
            for n in range(LAYERS):
                act.dma_start(layer[n][:, :], layer_params[n]).then_inc(params_in[n], 16)

            def qk_high(unit, half, before, ps=ps_misc):
                if half == 0 and before:
                    act.wait_ge(spread[before[0]], 16 * SPREADS * (before[1] + 1))
                act.wait_ge(qk_ready, 2 * unit + half + 1)
                act.activation(qk_hi[:, halves()[half]], ps[:, :], ACT.Identity,
                               bias=cur[:, BIAS_QK:BIAS_QK + 1]).then_inc(hi_done, 1)

            def place_k(unit, b, half):
                cols = halves()[half]
                act.wait_ge(hi_done, 2 * unit + half + 1)
                act.activation(k_twice[b][0:C, cols], qk_hi[C:P, cols].bitcast(F32), ACT.Copy)
                act.activation(k_twice[b][C:P, cols], qk_hi[C:P, cols].bitcast(F32), ACT.Copy).then_inc(k_placed, 1)

            def copy_v(unit, b, ps=ps_misc):
                act.wait_ge(v_ready, unit + 1)
                act.activation(vals[b][:, :], ps[:, 0:HALF], ACT.Copy).then_inc(v_copied, 1)

            def stage_max(unit, before):
                if before:
                    act.wait_ge(max_in[before[0]], 16 * (before[1] + 1))
                act.wait_ge(max_turned, unit + 1)
                act.activation(max_rows[:, :], ps_misc[0:TILES, 0:P], ACT.Copy).then_inc(max_staged, 1)

            def copy_den(unit):
                act.wait_ge(den_ready, unit + 1)
                act.wait_ge(rden_done, (unit + 1) * CHUNKS + 1)
                act.activation(den[:, :], ps_misc[:, :], ACT.Copy).then_inc(den_copied, 1)

            def exp(unit, t):
                act.wait_ge(scores_ready, TILES * unit + t + 1)
                act.wait_ge(probs_read, TILES * unit + t + 1)
                act.wait_ge(probs_added, ADDS * unit + max(t, 1))
                act.activation(probs[t][:, :], ps_scores[t % 2][:, :], ACT.Exp, scale=SCALE).then_inc(exp_done, 1)

            def copy_attn(unit, b):
                act.wait_ge(probs_read, TILES * (unit + 2))
                act.activation(attn[b][:, :], ps_attn[:, :], ACT.Copy).then_inc(attn_copied, 1)

            def window(w, r, i, prep, nxt, more):
                for t in range(TILES):
                    if t + 1 < TILES:
                        exp(w, t + 1)
                    elif more:
                        exp(w + 1, 0)
                    if t == 1:
                        if isinstance(w, int) or r:
                            copy_den(w - 1)
                        else:
                            with act.If(i > 0):
                                copy_den(w - 1)
                    if prep and t == 2:
                        qk_high(w + 2, 0, in_ring(r, i, 1))
                        place_k(w + 2, (r + 2) % RING, 0)
                    if prep and t == 3:
                        qk_high(w + 2, 1, None)
                        place_k(w + 2, (r + 2) % RING, 1)
                    if prep and t == 4:
                        copy_v(w + 2, (r + 2) % RING)
                    if nxt and t == 5:
                        stage_max(w + 1, in_ring(r, i, 0))
                copy_attn(w, r)

            for u in range(2):
                qk_high(u, 0, (0, 0) if u else None)
                qk_high(u, 1, None, ps_attn)
                place_k(u, u, 0)
                place_k(u, u, 1)
                copy_v(u, u, (ps_max, ps_misc)[u])
            stage_max(0, None)
            exp(0, 0)
            with act.Fori(0, LAST_LOOP // RING) as i:
                for r in range(RING):
                    window(i * RING + r, r, i, True, True, True)
            for w in range(LAST_LOOP, UNITS):
                window(w, w % RING, w // RING, False, w + 1 < UNITS, w + 1 < UNITS)

        @block.vector
        def _(dve):

            def gn_stats(unit):
                dve.bn_stats(stats6[:, :], xs[:, slot(unit)]).then_inc(gn_step, 1)

            def gn_about(unit):
                dve.wait_ge(group_stat, 2 * unit + 1)
                dve.tensor_scalar(mean[:, :], ps_misc[:, 0:1], ps_misc[:, 1:2], None, ALU.add).then_inc(gn_step, 1)
                dve.wait_ge(gn_step, GN * unit + 2)
                dve.tensor_scalar(mean_dev[:, :], means, mean[:, :], None, ALU.subtract).then_inc(gn_step, 1)
                dve.wait_ge(gn_step, GN * unit + 3)
                dve.tensor_tensor(dev_sq[:, :], mean_dev[:, :], mean_dev[:, :], ALU.mult).then_inc(gn_step, 1)
                dve.wait_ge(gn_step, GN * unit + 4)
                dve.scalar_tensor_tensor(out=var_about[:, :], in0=sq_devs, scalar=2.0 / HALF, in1=dev_sq[:, :],
                                         op0=ALU.mult, op1=ALU.add).then_inc(gn_step, 1)

            def gn_var(unit):
                dve.wait_ge(group_stat, 2 * unit + 2)
                dve.tensor_scalar(var_eps[:, :], ps_misc[:, 2:3], ps_misc[:, 3:4], cur[:, EPS:EPS + 1],
                                  ALU.add, ALU.add).then_inc(var_ready, 1)

            def gn_apply(unit):
                dve.wait_ge(rstd_ready, unit + 1)
                dve.tensor_tensor(gain[:, :], rstd[:, :], cur[:, NORM_W:NORM_W + 1], ALU.mult).then_inc(gn_step, 1)
                dve.wait_ge(gn_step, GN * unit + 6)
                dve.scalar_tensor_tensor(out=neg_shift[:, :], in0=mean[:, :], scalar=gain[:, :],
                                         in1=cur[:, NORM_B:NORM_B + 1], op0=ALU.mult, op1=ALU.subtract).then_inc(gn_step, 1)
                dve.wait_ge(gn_step, GN * unit + 7)
                dve.wait_ge(v_copied, unit)
                dve.tensor_scalar(h[:, :], xs[:, slot(unit)], gain[:, :], neg_shift[:, :],
                                  ALU.mult, ALU.subtract).then_inc(gn_step, 1)

            def qk_low(unit, half, ps=ps_misc):
                cols = halves()[half]
                dve.wait_ge(hi_done, 2 * unit + half + 1)
                dve.scalar_tensor_tensor(out=qk_lo[:, cols], in0=ps[:, :], scalar=cur[:, BIAS_QK:BIAS_QK + 1],
                                         in1=qk_hi[:, cols].bitcast(F32), op0=ALU.add,
                                         op1=ALU.subtract).then_inc(lo_done, 1)

            def row_max(unit, b, t, ps=ps_max):
                dve.wait_ge(max_mm, TILES * unit + t + 1)
                dve.tensor_reduce(neg_max[b][:, t:t + 1], ps[:, :], AX.X, ALU.max, negate=True).then_inc(max_done, 1)

            def reciprocal(unit, chunk):
                cols = slice(chunk * HALF // CHUNKS, (chunk + 1) * HALF // CHUNKS)
                if chunk == 0:
                    dve.wait_ge(den_copied, unit + 2)
                dve.reciprocal(rden[:, cols], den[:, cols]).then_inc(rden_done, 1)

            def final(unit, b, part):
                cols = slice(part * HALF // 2, (part + 1) * HALF // 2)
                dve.wait_ge(attn_copied, unit + 2)
                dve.wait_ge(rden_done, (unit + 1) * CHUNKS + (part + 1) * CHUNKS // 2 + 1)
                dve.tensor_tensor(scaled[:, cols], attn[b][:, cols], rden[:, cols], ALU.mult).then_inc(scaled_done, 1)
                dve.wait_ge(scaled_done, 2 * (unit + 1) + part + 1)
                dve.scalar_tensor_tensor(out=xs[:, slot_part(unit + B, part)], in0=scaled[:, cols],
                                         scalar=out_const[:, bass.ds(unit + 1, 1)], in1=xs[:, slot_part(unit, part)],
                                         op0=ALU.add, op1=ALU.add).then_inc(final_done, 1)

            def add_last(unit, b, t):
                dve.wait_ge(exp_done, TILES * unit + t + 2)
                dve.wait_ge(probs_added, ADDS * (unit + 1) + t - 1)
                first = probs[0] if t == 1 else prob_sum[b]
                dve.tensor_tensor(prob_sum[b][:, :], first[:, :], probs[t][:, :], ALU.add).then_inc(probs_added, 1)

            def finish_last(unit, b):
                dve.wait_ge(den_ready, unit + 1)
                dve.wait_ge(attn_copied, unit + 2)
                for chunk in range(CHUNKS):
                    cols = slice(chunk * HALF // CHUNKS, (chunk + 1) * HALF // CHUNKS)
                    at = (unit + 1) * HALF + cols.start
                    dve.reciprocal(rden[:, cols], ps_misc[:, cols]).then_inc(rden_done, 1)
                    dve.wait_ge(rden_done, (unit + 1) * CHUNKS + chunk + 2)
                    dve.tensor_tensor(scaled[:, cols], attn[b][:, cols], rden[:, cols], ALU.mult).then_inc(scaled_done, 1)
                    dve.wait_ge(scaled_done, 2 * (unit + 1) + chunk + 1)
                    dve.scalar_tensor_tensor(out=xs[:, at + B * HALF:at + B * HALF + HALF // CHUNKS],
                                             in0=scaled[:, cols], scalar=out_const[:, unit + 1:unit + 2],
                                             in1=xs[:, at:at + HALF // CHUNKS],
                                             op0=ALU.add, op1=ALU.add).then_inc(final_done, 1)

            def finish(unit, b, t):
                if 2 <= t < 2 + CHUNKS:
                    reciprocal(unit, t - 2)
                if t == 4:
                    final(unit, b, 0)
                if t == 6:
                    final(unit, b, 1)

            def window(w, r, i, prep, nxt):
                if prep and r == RING - 1:
                    dve.wait_ge(v_copied, w + 2)
                    dve.wait_ge(setup_done, 2 * LAYERS)
                    dve.tensor_copy(cur[:, 0:UNIT_COLS], layer[1][:, 0:UNIT_COLS]).then_inc(layer_switched, 1)
                for t in range(TILES):
                    m = t + MAX_LEAD
                    if prep and t == 0:
                        gn_stats(w + 2)
                    if prep and t == 1:
                        gn_var(w + 2)
                    if prep and t == 3:
                        qk_low(w + 2, 0)
                    if t == 2 or t == 5:
                        if isinstance(w, int) or r:
                            finish(w - 1, (r - 1) % RING, t)
                        else:
                            with dve.If(i > 0):
                                finish(w - 1, (r - 1) % RING, t)
                    if m < TILES and nxt:
                        row_max(w + 1, (r + 1) % RING, m)
                    elif m >= TILES and prep:
                        row_max(w + 2, (r + 2) % RING, m - TILES)
                    if t in (3, 4, 6):
                        if isinstance(w, int) or r:
                            finish(w - 1, (r - 1) % RING, t)
                        else:
                            with dve.If(i > 0):
                                finish(w - 1, (r - 1) % RING, t)
                    if isinstance(w, int) and w == UNITS - 1 and 1 <= t < TILES - 1:
                        add_last(w, r, t)
                    if prep and t == 0:
                        if r == RING - 1:
                            dve.wait_ge(layer_switched, i + 1)
                        gn_about(w + 2)
                    if prep and t == 1:
                        gn_apply(w + 2)
                    if prep and t == 3:
                        qk_low(w + 2, 1)
                dve.wait_ge(final_done, 2 * w + 1)

            def set_eps(n):
                dve.wait_ge(params_in[n], 16)
                dve.memset(layer[n][:, EPS:EPS + 1], (1e-5, 1e-6)[n]).then_inc(setup_done, 1)

            def setup(n):
                dve.wait_ge(setup_mm, n + 1)
                dve.wait_ge(params_in[n], 16)
                for half in range(2):
                    rows = slice(half * C, half * C + C)
                    dve.tensor_copy(layer[n][rows, WVO + half * C:WVO + half * C + C], ps_attn[rows, 0:C])
                dve.tensor_scalar(out_const[:, n * B + 1:(n + 1) * B + 1], ones[:, 0:B], ps_attn[:, C:C + 1],
                                  layer[n][:, BIAS_O:BIAS_O + 1], ALU.mult, ALU.add).then_inc(setup_done, 1)

            starts = ((exp_done, 1), (attn_copied, 1), (den_copied, 1), (final_done, 1),
                      (rden_done, CHUNKS + 1), (scaled_done, 2))
            for n, (semaphore, value) in enumerate(starts):
                dve.memset(started[:, n:n + 1], 0.0).then_inc(semaphore, value)
            dve.wait_ge(x_in[0], 16)
            gn_stats(0)
            set_eps(0)
            gn_about(0)
            dve.wait_ge(probs_added, ADDS)
            dve.wait_ge(setup_done, 1)
            gn_var(0)
            setup(0)
            gn_apply(0)
            qk_low(0, 0)
            qk_low(0, 1, ps_attn)
            dve.wait_ge(x_in[1], 16)
            gn_stats(1)
            gn_about(1)
            gn_var(1)
            for t in range(TILES):
                row_max(0, 0, t, FIRST_MAX[t % 3])
                if t == 0:
                    gn_apply(1)
                if t == 2:
                    qk_low(1, 0)
                if t == 4:
                    qk_low(1, 1, ps_attn)
            set_eps(1)
            setup(1)
            for t in range(MAX_LEAD):
                row_max(1, 1, t)
            for b in range(2, B):
                dve.wait_ge(x_in[b], 16)
            with dve.Fori(0, LAST_LOOP // RING) as i:
                for r in range(RING):
                    window(i * RING + r, r, i, True, True)
            for w in range(LAST_LOOP, UNITS):
                window(w, w % RING, w // RING, False, w + 1 < UNITS)
            finish_last(UNITS - 1, (UNITS - 1) % RING)

        @block.tensor
        def _(pe):
            def group_mean_of(unit):
                pe.wait_ge(gn_step, GN * unit + 1)
                pe.matmul(ps_misc[:, 0:2], group_mean, means, start=True, stop=True).then_inc(group_stat, 1)

            def group_var_of(unit):
                pe.wait_ge(gn_step, GN * unit + 5)
                pe.matmul(ps_misc[:, 2:4], group_mean, var_about[:, :], start=True, stop=True).then_inc(group_stat, 1)

            def project_qk(unit, half, ps=ps_misc):
                if ps is ps_attn:
                    pe.wait_ge(setup_done, 2) if unit == 0 else pe.wait_ge(lo_done, 2)
                elif half == 0:
                    pe.wait_ge(gn_step, GN * unit + 8)
                else:
                    pe.wait_ge(lo_done, 2 * unit + 1)
                w = cur[:, (WA, WB)[half]:(WA, WB)[half] + P]
                pe.matmul(ps[:, :], w, h[:, :], start=True, stop=True).then_inc(qk_ready, 1)

            def project_v(unit, ps=ps_misc):
                if isinstance(unit, int) and unit < 2:
                    if unit:
                        pe.wait_ge(lo_done, 2 * unit + 1)
                else:
                    pe.wait_ge(lo_done, 2 * unit + 2)
                for j in range(HALF // P):
                    cols = slice(j * P, (j + 1) * P)
                    mm = pe.matmul(ps[:, cols], h[:, cols], cur[:, WVO:WVO + P], start=True, stop=True)
                mm.then_inc(v_ready, 1)

            def max_scores(unit, b, rounds, t):
                if t == 0:
                    pe.wait_ge(spread[b], 16 * SPREADS * (rounds + 1))
                    pe.wait_ge(k_placed, 2 * (unit + 1))
                ps = ps_max
                if isinstance(unit, int) and unit == 0:
                    ps = FIRST_MAX[t % 3]
                    if t == 2:
                        pe.wait_ge(v_copied, 1)
                    if t >= 3:
                        pe.wait_ge(max_done, t - 2)
                else:
                    pe.wait_ge(max_done, TILES * unit + t)
                for cols in halves():
                    mm = pe.matmul(ps[:, cols], q_both[b][:, t * P:(t + 1) * P], k_twice[b][:, cols],
                                   start=True, stop=True)
                mm.then_inc(max_mm, 1)

            def turn_max(unit, b):
                pe.wait_ge(max_done, TILES * (unit + 1))
                if not (isinstance(unit, int) and unit == 0):
                    pe.wait_ge(v_copied, min(unit + 2, UNITS) if isinstance(unit, int) else unit + 2)
                    pe.wait_ge(den_copied, unit)
                pe.transpose(ps_misc[0:TILES, 0:P], neg_max[b][:, :], ident).then_inc(max_turned, 1)

            def scores(unit, b, rounds, t):
                if t == 0:
                    pe.wait_ge(spread[b], 16 * SPREADS * (rounds + 1))
                    pe.wait_ge(max_in[b], 16 * (rounds + 1))
                if not (isinstance(unit, int) and unit == 0 and t < 2):
                    pe.wait_ge(exp_done, TILES * unit + t)
                keys = slice(t * P, (t + 1) * P)
                ps = ps_scores[t % 2]
                for cols in halves():
                    pe.matmul(ps[:, cols], k_twice[b][:, keys], q_both[b][:, cols], start=True, stop=False)
                for cols in halves():
                    mm = pe.matmul(ps[:, cols], k_low[b][:, keys], q_max[b][:, cols], start=False, stop=True)
                mm.then_inc(scores_ready, 1)

            def values(unit, b, t):
                if t == 0:
                    pe.wait_ge(v_copied, unit + 1)
                    pe.wait_ge(attn_copied, unit + 1)
                pe.wait_ge(exp_done, TILES * unit + t + 2)
                half, j = divmod(t, TILES // 2)
                v = vals[b][:, j * P + half * C:j * P + half * C + C]
                for n, cols in enumerate(halves()):
                    mm = pe.matmul(ps_attn[n * C:(n + 1) * C, :], v, probs[t][:, cols],
                                   start=(t == 0), stop=(t == TILES - 1))
                mm.then_inc(probs_read, 1)

            def denominators(unit, b):
                pe.wait_ge(probs_added, ADDS * (unit + 2))
                for n, cols in enumerate(halves()):
                    mm = pe.matmul(ps_misc[n * C:(n + 1) * C, :], ones[:, :], prob_sum[b][:, cols],
                                   start=True, stop=True)
                mm.then_inc(den_ready, 1)

            def denominators_last(unit, b, part):
                if part == 0:
                    pe.wait_ge(den_copied, UNITS)
                    pe.wait_ge(probs_added, ADDS * (unit + 2) - 1)
                summed = (prob_sum[b], probs[TILES - 1])[part]
                for n, cols in enumerate(halves()):
                    mm = pe.matmul(ps_misc[n * C:(n + 1) * C, :], ones[:, :], summed[:, cols],
                                   start=(part == 0), stop=(part == 1))
                if part == 1:
                    mm.then_inc(den_ready, 1)

            def window(w, r, i, prep, nxt):
                for t in range(TILES):
                    if t + 1 < TILES:
                        scores(w, *in_ring(r, i, 0), t + 1)
                    elif nxt:
                        scores(w + 1, *in_ring(r, i, 1), 0)
                    if prep and t == 1:
                        group_var_of(w + 2)
                    if prep and t == 3:
                        project_qk(w + 2, 1)
                    m = t + MAX_LEAD
                    if m < TILES and nxt:
                        max_scores(w + 1, *in_ring(r, i, 1), m)
                    elif m >= TILES and prep:
                        max_scores(w + 2, *in_ring(r, i, 2), m - TILES)
                    if prep and t == 0:
                        pe.wait_ge(max_staged, w + 1)
                        group_mean_of(w + 2)
                    if prep and t == 2:
                        pe.wait_ge(den_copied, w + 1)
                        project_qk(w + 2, 0)
                    if nxt and t == 5:
                        turn_max(w + 1, (r + 1) % RING)
                    if t == TILES - 1 and not nxt:
                        denominators_last(w, r, 0)
                    values(w, r, t)
                    if t == TILES - 1 and not nxt:
                        denominators_last(w, r, 1)
                    if t == 1:
                        if prep:
                            pe.wait_ge(var_ready, w + 3)
                        elif w < UNITS:
                            pe.wait_ge(max_staged, min(w + 1, UNITS))
                        if isinstance(w, int) or r:
                            denominators(w - 1, (r - 1) % RING)
                        else:
                            with pe.If(i > 0):
                                denominators(w - 1, (r - 1) % RING)
                    if prep and t == 4:
                        project_v(w + 2)

            def setup(n):
                p = layer[n]
                pe.wait_ge(params_in[n], 16)
                pe.matmul(ps_attn[:, 0:C], p[0:C, VAL_T:VAL_T + P], p[0:C, OUT_W:OUT_W + C], start=True, stop=True)
                pe.matmul(ps_attn[:, C:C + 1], p[0:C, OUT_W:OUT_W + P], p[0:C, BIAS_V:BIAS_V + 1],
                          start=True, stop=True).then_inc(setup_mm, 1)

            pe.wait_ge(consts_in, 16)
            group_mean_of(0)
            setup(0)
            group_var_of(0)
            project_qk(0, 0)
            project_qk(0, 1, ps_attn)
            project_v(0, ps_max)
            pe.wait_ge(lo_done, 1)
            group_mean_of(1)
            group_var_of(1)
            for t in range(TILES):
                max_scores(0, 0, 0, t)
                if t == 2:
                    project_qk(1, 0)
                if t == 3:
                    project_qk(1, 1, ps_attn)
                if t == 4:
                    project_v(1)
                if t == 6:
                    pe.wait_ge(lo_done, 4)
                    setup(1)
            pe.wait_ge(v_copied, 2)
            turn_max(0, 0)
            max_scores(1, 1, 0, 0)
            pe.wait_ge(rows_filled, 3 * RING)
            scores(0, 0, 0, 0)
            for t in range(1, MAX_LEAD):
                max_scores(1, 1, 0, t)
            pe.wait_ge(setup_done, 4)
            with pe.Fori(0, LAST_LOOP // RING) as i:
                for r in range(RING):
                    window(i * RING + r, r, i, True, True)
            for w in range(LAST_LOOP, UNITS):
                window(w, w % RING, w // RING, False, w + 1 < UNITS)



def pack_layer(np, wq, wk, bq, bk, v_rows, o_cols, bv, bo, norm_w, norm_b):
    C = wq.shape[0]
    p = np.zeros((P, LAYER_COLS), wq.dtype)
    for half, at in enumerate((WA, WB)):
        rows = slice(half * C, half * C + C)
        p[rows, at:at + C] = wq
        p[rows, at + C:at + P] = wk
        p[rows, NORM_W] = norm_w
        p[rows, NORM_B] = norm_b
        p[rows, BIAS_QK] = (bq, bk)[half]
        p[rows, BIAS_O] = bo
        p[0:C, VAL_T + half * C:VAL_T + half * C + C] = v_rows
        p[0:C, OUT_W + half * C:OUT_W + half * C + C] = o_cols
    p[0:C, BIAS_V] = bv
    return p


def kernel(**inputs):
    import numpy as np
    import concourse.bacc as bacc
    from concourse.bass_utils import run_bass_kernel_spmd

    a = {k: np.asarray(v) for k, v in inputs.items()}
    x = a["x"]
    B, C, H, W = x.shape
    half = H * W // 2
    xh = np.ascontiguousarray(x.reshape(B, C, 2, half).transpose(0, 2, 1, 3).reshape(B, 2 * C, half))
    g0 = lambda n: a["L0_conv_" + n]
    g1 = lambda n: a["L1_conv_" + n]
    layers = np.stack([
        pack_layer(np, g0("Wq"), g0("Wk"), g0("bq"), g0("bk"), g0("Wv").T, g0("Wo"), g0("bv"), g0("bo"),
                   g0("norm_w"), g0("norm_b")),
        pack_layer(np, g1("wq").T, g1("wk").T, g1("bq"), g1("bk"), g1("wv"), g1("wo").T, g1("bv"), g1("bo"),
                   g1("gamma"), g1("beta")),
    ])
    per_group = C // 32
    group = np.arange(P) % C // per_group
    consts = np.concatenate([np.eye(P), (group[:, None] == group[None, :]) / (4 * per_group)], 1).astype(np.float32)

    nc = bacc.Bacc("TRN2", target_bir_lowering=False, num_devices=1)
    arrays = {"x_dram": xh, "layers_dram": layers, "consts_dram": consts}
    aps = [nc.dram_tensor(k, v.shape, F32, kind="ExternalInput").ap() for k, v in arrays.items()]
    out = nc.dram_tensor("out_dram", xh.shape, F32, kind="ExternalOutput").ap()
    attention_pair(nc, *aps, out)
    r = run_bass_kernel_spmd(nc, [arrays], core_ids=[0])
    got = r.results[0]["out_dram"]
    return got.reshape(B, 2, C, half).transpose(0, 2, 1, 3).reshape(B, C, H, W)
```

```python
from contextlib import ExitStack

import concourse.bass as bass
from concourse import mybir

ALU = mybir.AluOpType
ACT = mybir.ActivationFunctionType
AX = mybir.AxisListType
F32 = mybir.dt.float32
F32R = mybir.dt.float32r

P = 128
WA, WB, WVO, NORM_W, NORM_B, BIAS_QK, EPS = 0, P, 2 * P, 3 * P, 3 * P + 1, 3 * P + 2, 3 * P + 3
UNIT_COLS = 3 * P + 4
VAL_T, OUT_W, BIAS_O, BIAS_V = UNIT_COLS, UNIT_COLS + P, UNIT_COLS + 2 * P, UNIT_COLS + 2 * P + 1
LAYER_COLS = UNIT_COLS + 2 * P + 2

LAYERS = 2
RING = 3
EARLY = 4
MAX_LEAD = 3


def attention_pair(nc, x, layer_params, consts, out):
    B, _, HALF = x.shape
    C = P // 2
    N = 2 * HALF
    TILES = N // P
    UNITS = LAYERS * B
    ADDS = TILES - 1
    SCALE = float(C) ** -0.5
    LAST_LOOP = UNITS - 2
    assert LAST_LOOP % RING == 0 and B == RING + 1

    with ExitStack() as ctx:
        def sb(name, shape, dt=F32):
            return ctx.enter_context(nc.sbuf_tensor(name, shape, dt))

        def psum(name, shape):
            return ctx.enter_context(nc.psum_tensor(name, shape, F32))

        def sem(name):
            return ctx.enter_context(nc.semaphore(name))

        xs = sb("xs", [P, ((LAYERS + 1) * B + 1) * HALF])
        layer = [sb(f"layer{n}", [P, LAYER_COLS]) for n in range(LAYERS)]
        cur = layer[0]
        const_sb = sb("const_sb", [P, 2 * P])
        ident, group_mean = const_sb[:, 0:P], const_sb[:, P:2 * P]
        ones = sb("ones", [P, C])
        started = sb("started", [P, 6])
        minus_half = sb("minus_half", [P, 1])
        out_const = sb("out_const", [P, UNITS + 1])

        stats6 = sb("stats6", [P, 6])
        means, sq_devs = stats6[:, 1::3], stats6[:, 2::3]
        mean = sb("mean", [P, 1])
        mean_dev = sb("mean_dev", [P, 2])
        dev_sq = sb("dev_sq", [P, 2])
        var_about = sb("var_about", [P, 2])
        var_eps = sb("var_eps", [P, 1])
        rstd = sb("rstd", [P, 1])
        gain = sb("gain", [P, 1])
        neg_shift = sb("neg_shift", [P, 1])
        h = sb("h", [P, HALF])
        qk_hi = sb("qk_hi", [P, N], F32R)
        q_both = [sb(f"q_both{b}", [P, N], F32R) for b in range(RING)]
        q_max = [sb(f"q_max{b}", [P, N], F32R) for b in range(RING)]
        k_twice = [sb(f"k_twice{b}", [P, N], F32R) for b in range(RING)]
        k_low = [sb(f"k_low{b}", [P, N], F32R) for b in range(RING)]
        vals = [sb(f"vals{b}", [P, HALF]) for b in range(RING)]
        neg_max = [sb(f"neg_max{b}", [P, TILES]) for b in range(RING)]
        max_rows = sb("max_rows", [TILES, P], F32R)
        probs = [sb(f"probs{t}", [P, N]) for t in range(TILES)]
        prob_sum = [sb(f"prob_sum{b}", [P, N]) for b in range(RING)]
        attn = [sb(f"attn{b}", [P, HALF]) for b in range(RING)]
        den = sb("den", [P, HALF])
        rden = sb("rden", [P, HALF])
        scaled = sb("scaled", [P, HALF])

        ps_scores = [psum(f"ps_scores{b}", [P, N]) for b in range(2)]
        ps_max = psum("ps_max", [P, N])
        ps_attn = psum("ps_attn", [P, HALF])
        ps_misc = psum("ps_misc", [P, HALF])

        x_in = [sem(f"x_in{b}") for b in range(B)]
        params_in = [sem(f"params_in{n}") for n in range(LAYERS)]
        consts_in = sem("consts_in")
        rows_filled = sem("rows_filled")
        setup_mm = sem("setup_mm")
        setup_done = sem("setup_done")
        gn_step = sem("gn_step")
        group_stat = sem("group_stat")
        var_ready = sem("var_ready")
        rstd_ready = sem("rstd_ready")
        qk_ready = sem("qk_ready")
        hi_done = sem("hi_done")
        placed = sem("placed")
        lo_done = sem("lo_done")
        v_ready = sem("v_ready")
        v_copied = sem("v_copied")
        max_mm = sem("max_mm")
        max_done = sem("max_done")
        max_turned = sem("max_turned")
        max_staged = sem("max_staged")
        max_in = [sem(f"max_in{b}") for b in range(RING)]
        scores_ready = sem("scores_ready")
        exp_done = sem("exp_done")
        probs_read = sem("probs_read")
        probs_added = sem("probs_added")
        late_added = sem("late_added")
        attn_copied = sem("attn_copied")
        den_ready = sem("den_ready")
        den_copied = sem("den_copied")
        rden_done = sem("rden_done")
        scaled_done = sem("scaled_done")
        final_done = sem("final_done")
        stored = sem("stored")
        layer_switched = sem("layer_switched")

        CHUNKS = 4
        GN = 8

        def slot(unit):
            return bass.ds((unit + 1) * HALF, HALF)

        def slot_part(unit, part):
            return bass.ds((unit + 1) * HALF + part * (HALF // 2), HALF // 2)

        FIRST_MAX = (ps_scores[0], ps_max)
        FIRST_QK = ((ps_misc, ps_attn), (ps_attn, ps_scores[1][:, HALF:N]))
        FIRST_V = (ps_scores[1][:, 0:HALF], ps_misc)

        def halves():
            return (slice(0, HALF), slice(HALF, N))

        block = ctx.enter_context(nc.Block())

        def in_ring(r, i, d):
            return (r + d) % RING, i + (r + d) // RING

        @block.sync
        def _(sp):
            for b in range(B):
                if b == 1:
                    sp.dma_start(const_sb[:, :], consts).then_inc(consts_in, 16)
                sp.dma_start(xs[:, (b + 1) * HALF:(b + 2) * HALF], x[b]).then_inc(x_in[b], 16)

            def place_max(unit, b):
                sp.wait_ge(max_staged, unit + 1)
                row = q_max[b][0:1, :].bitcast(F32).rearrange("p (t n) -> p t n", t=TILES)
                sp.dma_start(row, max_rows[:, :].bitcast(F32)).then_inc(max_in[b], 16)

            place_max(0, 0)
            with sp.Fori(0, LAST_LOOP // RING) as i:
                for r in range(RING):
                    place_max(i * RING + r + 1, (r + 1) % RING)
            place_max(UNITS - 1, (UNITS - 1) % RING)
            for image in range(B):
                unit = UNITS - B + image
                parts = 1 if unit < UNITS - 1 else CHUNKS
                for part in range(parts):
                    sp.wait_ge(final_done, 2 * (unit + 1) + 1 if parts == 1 else 2 * unit + part + 2)
                    cols = slice(part * HALF // parts, (part + 1) * HALF // parts)
                    src = xs[:, (unit + B + 1) * HALF + cols.start:(unit + B + 1) * HALF + cols.stop]
                    sp.dma_start(out[image, :, cols], src).then_inc(stored, 16)
            sp.wait_ge(stored, 16 * (B - 1 + CHUNKS))

        @block.gpsimd
        def _(pool):
            pool.memset(ones[:, :], 1.0).then_inc(probs_added, ADDS)
            pool.wait_ge(probs_added, ADDS)
            pool.memset(minus_half[:, :], -0.5).then_inc(probs_read, TILES)
            pool.wait_ge(probs_read, TILES)

            def root(unit):
                pool.wait_ge(var_ready, unit + 1)
                pool.tensor_tensor(rstd[:, :], var_eps[:, :], minus_half[:, :], ALU.pow).then_inc(rstd_ready, 1)

            def add(w, b, t):
                pool.wait_ge(exp_done, TILES * w + t + 2)
                first = probs[0] if t == 1 else prob_sum[b]
                pool.wait_ge(probs_added, ADDS * (w + 1) + t - 1)
                pool.tensor_tensor(prob_sum[b][:, :], first[:, :], probs[t][:, :], ALU.add).then_inc(probs_added, 1)

            def window(w, r, prep):
                for t in range(1, TILES):
                    add(w, r, t)
                    if t == 1 and prep:
                        root(w + 2)

            root(0)
            for b in range(RING):
                if b:
                    pool.wait_ge(rows_filled, 2 * b)
                else:
                    pool.wait_ge(rstd_ready, 1)
                pool.memset(k_low[b][0:C, :].bitcast(F32), 0.0).then_inc(rows_filled, 1)
                pool.wait_ge(rows_filled, 2 * b + 1)
                pool.memset(q_max[b][0:C, :].bitcast(F32), 0.0).then_inc(rows_filled, 1)
            pool.wait_ge(rows_filled, 2 * RING)
            root(1)
            pool.wait_ge(rstd_ready, 2)
            for b in range(RING):
                pool.memset(k_low[b][0:1, :].bitcast(F32), 1.0).then_inc(rows_filled, 1)
            pool.wait_ge(rows_filled, 3 * RING)
            with pool.Fori(0, LAST_LOOP // RING) as i:
                for r in range(RING):
                    window(i * RING + r, r, True)
            window(UNITS - 2, (UNITS - 2) % RING, False)
            for t in range(1, EARLY):
                add(UNITS - 1, (UNITS - 1) % RING, t)

        @block.scalar
        def _(act):
            for n in range(LAYERS):
                act.dma_start(layer[n][:, :], layer_params[n]).then_inc(params_in[n], 16)

            def qk_high(unit, b, half, ps=ps_misc):
                act.wait_ge(qk_ready, 2 * unit + half + 1)
                act.activation(qk_hi[:, halves()[half]], ps[:, :], ACT.Identity,
                               bias=cur[:, BIAS_QK:BIAS_QK + 1]).then_inc(hi_done, 1)

            def place_k(unit, b, half):
                cols = halves()[half]
                act.wait_ge(hi_done, 2 * unit + half + 1)
                act.activation(k_twice[b][0:C, cols], qk_hi[C:P, cols].bitcast(F32), ACT.Copy)
                act.activation(k_twice[b][C:P, cols], qk_hi[C:P, cols].bitcast(F32), ACT.Copy).then_inc(placed, 1)

            def place_q(unit, b, place):
                act.wait_ge(hi_done, 2 * unit + 2)
                act.activation(place[b][C:P, :], qk_hi[0:C, :].bitcast(F32), ACT.Copy).then_inc(placed, 1)

            def copy_v(unit, b, ps=ps_misc):
                act.wait_ge(v_ready, unit + 1)
                act.activation(vals[b][:, :], ps[:, 0:HALF], ACT.Copy).then_inc(v_copied, 1)

            def stage_max(unit, before):
                if before:
                    act.wait_ge(max_in[before[0]], 16 * (before[1] + 1))
                act.wait_ge(max_turned, unit + 1)
                act.activation(max_rows[:, :], ps_misc[0:TILES, 0:P], ACT.Copy).then_inc(max_staged, 1)

            def copy_den(unit):
                act.wait_ge(den_ready, unit + 1)
                act.wait_ge(rden_done, (unit + 1) * CHUNKS + 1)
                act.activation(den[:, :], ps_misc[:, :], ACT.Copy).then_inc(den_copied, 1)

            def exp(unit, t):
                act.wait_ge(scores_ready, TILES * unit + t + 1)
                act.wait_ge(probs_read, TILES * unit + t + 1)
                act.wait_ge(probs_added, ADDS * unit + max(t, 1))
                act.activation(probs[t][:, :], ps_scores[t % 2][:, :], ACT.Exp, scale=SCALE).then_inc(exp_done, 1)

            def copy_attn(unit, b):
                act.wait_ge(probs_read, TILES * (unit + 2))
                act.activation(attn[b][:, :], ps_attn[:, :], ACT.Copy).then_inc(attn_copied, 1)

            def window(w, r, i, prep, nxt):
                def exp_next(t):
                    if t + 1 < TILES:
                        exp(w, t + 1)
                    elif nxt:
                        exp(w + 1, 0)

                def copy_den_before():
                    if isinstance(w, int) or r:
                        copy_den(w - 1)
                    else:
                        with act.If(i > 0):
                            copy_den(w - 1)

                def for_unit_after_next(step, *args):
                    if prep:
                        step(w + 2, (r + 2) % RING, *args)

                exp_next(0)
                exp_next(1)
                copy_den_before()
                exp_next(2)
                for_unit_after_next(qk_high, 0)
                for_unit_after_next(place_k, 0)
                for_unit_after_next(qk_high, 1)
                exp_next(3)
                for_unit_after_next(place_k, 1)
                for_unit_after_next(place_q, q_both)
                exp_next(4)
                for_unit_after_next(copy_v)
                for_unit_after_next(place_q, q_max)
                if nxt:
                    stage_max(w + 1, in_ring(r, i, 0))
                exp_next(5)
                exp_next(6)
                exp_next(7)
                copy_attn(w, r)

            for u in range(2):
                for half in range(2):
                    qk_high(u, u, half, FIRST_QK[u][half])
                    place_k(u, u, half)
                place_q(u, u, q_both)
                place_q(u, u, q_max)
                copy_v(u, u, FIRST_V[u])
            stage_max(0, None)
            exp(0, 0)
            with act.Fori(0, LAST_LOOP // RING) as i:
                for r in range(RING):
                    window(i * RING + r, r, i, True, True)
            for w in range(LAST_LOOP, UNITS):
                window(w, w % RING, w // RING, False, w + 1 < UNITS)

        @block.vector
        def _(dve):

            def gn_stats(unit):
                dve.bn_stats(stats6[:, :], xs[:, slot(unit)]).then_inc(gn_step, 1)

            def gn_about(unit):
                dve.wait_ge(group_stat, 2 * unit + 1)
                dve.tensor_scalar(mean[:, :], ps_misc[:, 0:1], ps_misc[:, 1:2], None, ALU.add).then_inc(gn_step, 1)
                dve.wait_ge(gn_step, GN * unit + 2)
                dve.tensor_scalar(mean_dev[:, :], means, mean[:, :], None, ALU.subtract).then_inc(gn_step, 1)
                dve.wait_ge(gn_step, GN * unit + 3)
                dve.tensor_tensor(dev_sq[:, :], mean_dev[:, :], mean_dev[:, :], ALU.mult).then_inc(gn_step, 1)
                dve.wait_ge(gn_step, GN * unit + 4)
                dve.scalar_tensor_tensor(out=var_about[:, :], in0=sq_devs, scalar=2.0 / HALF, in1=dev_sq[:, :],
                                         op0=ALU.mult, op1=ALU.add).then_inc(gn_step, 1)

            def gn_var(unit):
                dve.wait_ge(group_stat, 2 * unit + 2)
                dve.tensor_scalar(var_eps[:, :], ps_misc[:, 2:3], ps_misc[:, 3:4], cur[:, EPS:EPS + 1],
                                  ALU.add, ALU.add).then_inc(var_ready, 1)

            def gn_apply(unit):
                dve.wait_ge(rstd_ready, unit + 1)
                dve.tensor_tensor(gain[:, :], rstd[:, :], cur[:, NORM_W:NORM_W + 1], ALU.mult).then_inc(gn_step, 1)
                dve.wait_ge(gn_step, GN * unit + 6)
                dve.scalar_tensor_tensor(out=neg_shift[:, :], in0=mean[:, :], scalar=gain[:, :],
                                         in1=cur[:, NORM_B:NORM_B + 1], op0=ALU.mult, op1=ALU.subtract).then_inc(gn_step, 1)
                dve.wait_ge(gn_step, GN * unit + 7)
                dve.wait_ge(v_copied, unit)
                dve.tensor_scalar(h[:, :], xs[:, slot(unit)], gain[:, :], neg_shift[:, :],
                                  ALU.mult, ALU.subtract).then_inc(gn_step, 1)

            def qk_low(unit, b, half, ps=ps_misc):
                cols = halves()[half]
                dve.wait_ge(hi_done, 2 * unit + half + 1)
                for rows, low in ((slice(0, C), q_both[b]), (slice(C, P), k_low[b])):
                    op = dve.scalar_tensor_tensor(out=low[rows, cols], in0=ps[rows, :],
                                                  scalar=cur[rows, BIAS_QK:BIAS_QK + 1],
                                                  in1=qk_hi[rows, cols].bitcast(F32), op0=ALU.add,
                                                  op1=ALU.subtract)
                op.then_inc(lo_done, 1)

            def row_max(unit, b, t, ps=ps_max):
                dve.wait_ge(max_mm, TILES * unit + t + 1)
                dve.tensor_reduce(neg_max[b][:, t:t + 1], ps[:, :], AX.X, ALU.max, negate=True).then_inc(max_done, 1)

            def reciprocal(unit, chunk):
                cols = slice(chunk * HALF // CHUNKS, (chunk + 1) * HALF // CHUNKS)
                if chunk == 0:
                    dve.wait_ge(den_copied, unit + 2)
                dve.reciprocal(rden[:, cols], den[:, cols]).then_inc(rden_done, 1)

            def final(unit, b, part):
                cols = slice(part * HALF // 2, (part + 1) * HALF // 2)
                dve.wait_ge(attn_copied, unit + 2)
                dve.wait_ge(rden_done, (unit + 1) * CHUNKS + (part + 1) * CHUNKS // 2 + 1)
                dve.tensor_tensor(scaled[:, cols], attn[b][:, cols], rden[:, cols], ALU.mult).then_inc(scaled_done, 1)
                dve.wait_ge(scaled_done, 2 * (unit + 1) + part + 1)
                dve.scalar_tensor_tensor(out=xs[:, slot_part(unit + B, part)], in0=scaled[:, cols],
                                         scalar=out_const[:, bass.ds(unit + 1, 1)], in1=xs[:, slot_part(unit, part)],
                                         op0=ALU.add, op1=ALU.add).then_inc(final_done, 1)

            def add_late(unit, b, t):
                late = prob_sum[(b + 1) % RING]
                dve.wait_ge(exp_done, TILES * unit + t + 2)
                if t > EARLY + 1:
                    dve.wait_ge(late_added, t - EARLY - 1)
                first = probs[EARLY] if t == EARLY + 1 else late
                dve.tensor_tensor(late[:, :], first[:, :], probs[t][:, :], ALU.add).then_inc(late_added, 1)

            def finish_last(unit, b):
                chunks = [slice(c * HALF // CHUNKS, (c + 1) * HALF // CHUNKS) for c in range(CHUNKS)]
                dve.wait_ge(den_ready, unit + 1)
                for c in range(2):
                    dve.reciprocal(rden[:, chunks[c]], ps_misc[:, chunks[c]]).then_inc(rden_done, 1)
                for c, cols in enumerate(chunks):
                    at = (unit + 1) * HALF + cols.start
                    if c == 0:
                        dve.wait_ge(attn_copied, unit + 2)
                    dve.wait_ge(rden_done, (unit + 1) * CHUNKS + c + 2)
                    dve.tensor_tensor(scaled[:, cols], attn[b][:, cols], rden[:, cols], ALU.mult).then_inc(scaled_done, 1)
                    if c + 2 < CHUNKS:
                        dve.reciprocal(rden[:, chunks[c + 2]], ps_misc[:, chunks[c + 2]]).then_inc(rden_done, 1)
                    dve.wait_ge(scaled_done, 2 * (unit + 1) + c + 1)
                    dve.scalar_tensor_tensor(out=xs[:, at + B * HALF:at + B * HALF + HALF // CHUNKS],
                                             in0=scaled[:, cols], scalar=out_const[:, unit + 1:unit + 2],
                                             in1=xs[:, at:at + HALF // CHUNKS],
                                             op0=ALU.add, op1=ALU.add).then_inc(final_done, 1)

            def window(w, r, i, prep, nxt):
                if prep and r == RING - 1:
                    dve.wait_ge(v_copied, w + 2)
                    dve.wait_ge(setup_done, 2 * LAYERS)
                    dve.tensor_copy(cur[:, 0:UNIT_COLS], layer[1][:, 0:UNIT_COLS]).then_inc(layer_switched, 1)
                def next_max(t):
                    m = t + MAX_LEAD
                    if m < TILES and nxt:
                        row_max(w + 1, (r + 1) % RING, m)
                    elif m >= TILES and prep:
                        row_max(w + 2, (r + 2) % RING, m - TILES)
                    if isinstance(w, int) and w == UNITS - 1 and EARLY < t < TILES - 1:
                        add_late(w, r, t)

                def for_unit_before(step, *args):
                    if isinstance(w, int) or r:
                        step(w - 1, *args)
                    else:
                        with dve.If(i > 0):
                            step(w - 1, *args)

                def for_unit_after_next(step, *args):
                    if prep:
                        step(w + 2, *args)

                for_unit_after_next(gn_stats)
                next_max(0)
                if prep and r == RING - 1:
                    dve.wait_ge(layer_switched, i + 1)
                for_unit_after_next(gn_about)
                for_unit_after_next(gn_var)
                next_max(1)
                for_unit_after_next(gn_apply)
                for_unit_before(reciprocal, 0)
                next_max(2)
                for_unit_after_next(qk_low, (r + 2) % RING, 0)
                next_max(3)
                for_unit_before(reciprocal, 1)
                for_unit_after_next(qk_low, (r + 2) % RING, 1)
                next_max(4)
                for_unit_before(reciprocal, 2)
                for_unit_before(final, (r - 1) % RING, 0)
                next_max(5)
                for_unit_before(reciprocal, 3)
                next_max(6)
                for_unit_before(final, (r - 1) % RING, 1)
                next_max(7)
                dve.wait_ge(final_done, 2 * w + 1)

            def set_eps(n):
                dve.wait_ge(params_in[n], 16)
                dve.memset(layer[n][:, EPS:EPS + 1], (1e-5, 1e-6)[n]).then_inc(setup_done, 1)

            def setup(n):
                dve.wait_ge(setup_mm, n + 1)
                dve.wait_ge(params_in[n], 16)
                for half in range(2):
                    rows = slice(half * C, half * C + C)
                    dve.tensor_copy(layer[n][rows, WVO + half * C:WVO + half * C + C], ps_attn[rows, 0:C])
                dve.tensor_scalar(out_const[:, n * B + 1:(n + 1) * B + 1], ones[:, 0:B], ps_attn[:, C:C + 1],
                                  layer[n][:, BIAS_O:BIAS_O + 1], ALU.mult, ALU.add).then_inc(setup_done, 1)

            starts = ((exp_done, 1), (attn_copied, 1), (den_copied, 1), (final_done, 1),
                      (rden_done, CHUNKS + 1), (scaled_done, 2))
            for n, (semaphore, value) in enumerate(starts):
                dve.memset(started[:, n:n + 1], 0.0).then_inc(semaphore, value)
            dve.wait_ge(x_in[0], 16)
            gn_stats(0)
            set_eps(0)
            gn_about(0)
            dve.wait_ge(probs_added, ADDS)
            dve.wait_ge(setup_done, 1)
            gn_var(0)
            setup(0)
            gn_apply(0)
            for half in range(2):
                qk_low(0, 0, half, FIRST_QK[0][half])
            dve.wait_ge(x_in[1], 16)
            gn_stats(1)
            gn_about(1)
            set_eps(1)
            for t in range(TILES):
                row_max(0, 0, t, FIRST_MAX[t % 2])
                if t == 0:
                    gn_var(1)
                    setup(1)
                if t == 1:
                    gn_apply(1)
            for half in range(2):
                qk_low(1, 1, half, FIRST_QK[1][half])
            for t in range(MAX_LEAD):
                row_max(1, 1, t, (ps_max, ps_scores[1], ps_max)[t])
            for b in range(2, B):
                dve.wait_ge(x_in[b], 16)
            with dve.Fori(0, LAST_LOOP // RING) as i:
                for r in range(RING):
                    window(i * RING + r, r, i, True, True)
            for w in range(LAST_LOOP, UNITS):
                window(w, w % RING, w // RING, False, w + 1 < UNITS)
            finish_last(UNITS - 1, (UNITS - 1) % RING)

        @block.tensor
        def _(pe):
            def group_mean_of(unit):
                pe.wait_ge(gn_step, GN * unit + 1)
                pe.matmul(ps_misc[:, 0:2], group_mean, means, start=True, stop=True).then_inc(group_stat, 1)

            def group_var_of(unit):
                pe.wait_ge(gn_step, GN * unit + 5)
                pe.matmul(ps_misc[:, 2:4], group_mean, var_about[:, :], start=True, stop=True).then_inc(group_stat, 1)

            def project_qk(unit, half, ps=ps_misc):
                pe.wait_ge(gn_step, GN * unit + 8)
                w = cur[:, (WA, WB)[half]:(WA, WB)[half] + P]
                pe.matmul(ps[:, :], w, h[:, :], start=True, stop=True).then_inc(qk_ready, 1)

            def project_v(unit, ps=ps_misc):
                for j in range(HALF // P):
                    cols = slice(j * P, (j + 1) * P)
                    mm = pe.matmul(ps[:, cols], h[:, cols], cur[:, WVO:WVO + P], start=True, stop=True)
                mm.then_inc(v_ready, 1)

            def max_scores(unit, b, rounds, t):
                if t == 0:
                    pe.wait_ge(placed, 4 * unit + 3)
                    pe.wait_ge(lo_done, 2 * (unit + 1))
                ps = ps_max
                if isinstance(unit, int) and unit == 0:
                    ps = FIRST_MAX[t % 2]
                    if t >= 2:
                        pe.wait_ge(max_done, t - 1)
                elif isinstance(unit, int) and unit == 1 and t == 1:
                    ps = ps_scores[1]
                else:
                    pe.wait_ge(max_done, TILES * unit + t)
                for cols in halves():
                    mm = pe.matmul(ps[:, cols], q_both[b][:, t * P:(t + 1) * P], k_twice[b][:, cols],
                                   start=True, stop=True)
                mm.then_inc(max_mm, 1)

            def turn_max(unit, b):
                pe.wait_ge(max_done, TILES * (unit + 1))
                pe.wait_ge(v_copied, min(unit + 2, UNITS) if isinstance(unit, int) else unit + 2)
                if not (isinstance(unit, int) and unit == 0):
                    pe.wait_ge(den_copied, unit)
                pe.transpose(ps_misc[0:TILES, 0:P], neg_max[b][:, :], ident).then_inc(max_turned, 1)

            def scores(unit, b, rounds, t):
                if t == 0:
                    pe.wait_ge(placed, 4 * (unit + 1))
                    pe.wait_ge(max_in[b], 16 * (rounds + 1))
                if not (isinstance(unit, int) and unit == 0 and t < 2):
                    pe.wait_ge(exp_done, TILES * unit + t)
                keys = slice(t * P, (t + 1) * P)
                ps = ps_scores[t % 2]
                for cols in halves():
                    pe.matmul(ps[:, cols], k_twice[b][:, keys], q_both[b][:, cols], start=True, stop=False)
                for cols in halves():
                    mm = pe.matmul(ps[:, cols], k_low[b][:, keys], q_max[b][:, cols], start=False, stop=True)
                mm.then_inc(scores_ready, 1)

            def values(unit, b, t):
                if t == 0:
                    pe.wait_ge(v_copied, unit + 1)
                    pe.wait_ge(attn_copied, unit + 1)
                pe.wait_ge(exp_done, TILES * unit + t + 2)
                half, j = divmod(t, TILES // 2)
                v = vals[b][:, j * P + half * C:j * P + half * C + C]
                for n, cols in enumerate(halves()):
                    mm = pe.matmul(ps_attn[n * C:(n + 1) * C, :], v, probs[t][:, cols],
                                   start=(t == 0), stop=(t == TILES - 1))
                mm.then_inc(probs_read, 1)

            def denominators(unit, b):
                pe.wait_ge(probs_added, ADDS * (unit + 2))
                for n, cols in enumerate(halves()):
                    mm = pe.matmul(ps_misc[n * C:(n + 1) * C, :], ones[:, :], prob_sum[b][:, cols],
                                   start=True, stop=True)
                mm.then_inc(den_ready, 1)

            def denominators_last(unit, b, part):
                if part == 0:
                    pe.wait_ge(den_copied, UNITS)
                    pe.wait_ge(probs_added, ADDS * (unit + 1) + EARLY - 1)
                elif part == 1:
                    pe.wait_ge(late_added, TILES - EARLY - 2)
                else:
                    pe.wait_ge(exp_done, TILES * (unit + 1) + 1)
                summed = (prob_sum[b], prob_sum[(b + 1) % RING], probs[TILES - 1])[part]
                for n, cols in enumerate(halves()):
                    mm = pe.matmul(ps_misc[n * C:(n + 1) * C, :], ones[:, :], summed[:, cols],
                                   start=(part == 0), stop=(part == 2))
                if part == 2:
                    mm.then_inc(den_ready, 1)

            def window(w, r, i, prep, nxt):
                def next_scores(t):
                    if t + 1 < TILES:
                        scores(w, *in_ring(r, i, 0), t + 1)
                    elif nxt:
                        scores(w + 1, *in_ring(r, i, 1), 0)

                def next_max(t):
                    m = t + MAX_LEAD
                    if m < TILES and nxt:
                        max_scores(w + 1, *in_ring(r, i, 1), m)
                    elif m >= TILES and prep:
                        max_scores(w + 2, *in_ring(r, i, 2), m - TILES)

                def denominators_before():
                    if prep:
                        pe.wait_ge(var_ready, w + 3)
                    else:
                        pe.wait_ge(max_staged, min(w + 1, UNITS))
                    if isinstance(w, int) or r:
                        denominators(w - 1, (r - 1) % RING)
                    else:
                        with pe.If(i > 0):
                            denominators(w - 1, (r - 1) % RING)

                next_scores(0)
                next_max(0)
                next_scores(1)
                if prep:
                    pe.wait_ge(max_staged, w + 1)
                    group_mean_of(w + 2)
                values(w, r, 0)
                next_max(1)
                if prep:
                    group_var_of(w + 2)
                values(w, r, 1)
                denominators_before()
                next_scores(2)
                next_max(2)
                if prep:
                    pe.wait_ge(den_copied, w + 1)
                    project_qk(w + 2, 0)
                next_scores(3)
                values(w, r, 2)
                next_max(3)
                if prep:
                    pe.wait_ge(lo_done, 2 * (w + 2) + 1)
                    project_qk(w + 2, 1)
                values(w, r, 3)
                next_scores(4)
                next_max(4)
                values(w, r, 4)
                if prep:
                    pe.wait_ge(lo_done, 2 * (w + 2) + 2)
                    project_v(w + 2)
                next_max(5)
                next_scores(5)
                if nxt:
                    turn_max(w + 1, (r + 1) % RING)
                next_scores(6)
                values(w, r, 5)
                if not nxt:
                    denominators_last(w, r, 0)
                next_max(6)
                values(w, r, 6)
                next_scores(7)
                next_max(7)
                if not nxt:
                    denominators_last(w, r, 1)
                    denominators_last(w, r, 2)
                values(w, r, 7)

            def keep_warm(times, ps=ps_scores[0]):
                for _ in range(times):
                    pe.matmul(ps[0:C, 0:C], ones[:, :], ones[:, :], start=True, stop=True)

            def setup(n):
                p = layer[n]
                pe.wait_ge(params_in[n], 16)
                pe.matmul(ps_attn[:, 0:C], p[0:C, VAL_T:VAL_T + P], p[0:C, OUT_W:OUT_W + C], start=True, stop=True)
                pe.matmul(ps_attn[:, C:C + 1], p[0:C, OUT_W:OUT_W + P], p[0:C, BIAS_V:BIAS_V + 1],
                          start=True, stop=True).then_inc(setup_mm, 1)

            pe.wait_ge(probs_added, ADDS)
            keep_warm(17)
            pe.wait_ge(consts_in, 16)
            group_mean_of(0)
            setup(0)
            keep_warm(3)
            group_var_of(0)
            keep_warm(9)
            pe.wait_ge(setup_done, 2)
            for half in range(2):
                project_qk(0, half, FIRST_QK[0][half])
            project_v(0, FIRST_V[0])
            pe.wait_ge(lo_done, 1)
            keep_warm(10)
            group_mean_of(1)
            for t in range(TILES):
                max_scores(0, 0, 0, t)
                if t == 1:
                    group_var_of(1)
                    setup(1)
                if t in (1, 2):
                    pe.wait_ge(v_copied, 1)
                    keep_warm(8, ps_scores[1])
                if t == 3:
                    pe.wait_ge(setup_done, 4)
                    project_qk(1, 0, FIRST_QK[1][0])
                if t == 4:
                    project_qk(1, 1, FIRST_QK[1][1])
                if t == 5:
                    project_v(1, FIRST_V[1])
            turn_max(0, 0)
            keep_warm(14)
            max_scores(1, 1, 0, 0)
            pe.wait_ge(rows_filled, 3 * RING)
            scores(0, 0, 0, 0)
            for t in range(1, MAX_LEAD):
                max_scores(1, 1, 0, t)
            pe.wait_ge(max_done, TILES + 2)
            with pe.Fori(0, LAST_LOOP // RING) as i:
                for r in range(RING):
                    window(i * RING + r, r, i, True, True)
            for w in range(LAST_LOOP, UNITS):
                window(w, w % RING, w // RING, False, w + 1 < UNITS)



def pack_layer(np, wq, wk, bq, bk, v_rows, o_cols, bv, bo, norm_w, norm_b):
    C = wq.shape[0]
    p = np.zeros((P, LAYER_COLS), wq.dtype)
    for half, at in enumerate((WA, WB)):
        rows = slice(half * C, half * C + C)
        p[rows, at:at + C] = wq
        p[rows, at + C:at + P] = wk
        p[rows, NORM_W] = norm_w
        p[rows, NORM_B] = norm_b
        p[rows, BIAS_QK] = (bq, bk)[half]
        p[rows, BIAS_O] = bo
        p[0:C, VAL_T + half * C:VAL_T + half * C + C] = v_rows
        p[0:C, OUT_W + half * C:OUT_W + half * C + C] = o_cols
    p[0:C, BIAS_V] = bv
    return p


def kernel(**inputs):
    import numpy as np
    import concourse.bacc as bacc
    from concourse.bass_utils import run_bass_kernel_spmd

    a = {k: np.asarray(v) for k, v in inputs.items()}
    x = a["x"]
    B, C, H, W = x.shape
    half = H * W // 2
    xh = np.ascontiguousarray(x.reshape(B, C, 2, half).transpose(0, 2, 1, 3).reshape(B, 2 * C, half))
    g0 = lambda n: a["L0_conv_" + n]
    g1 = lambda n: a["L1_conv_" + n]
    layers = np.stack([
        pack_layer(np, g0("Wq"), g0("Wk"), g0("bq"), g0("bk"), g0("Wv").T, g0("Wo"), g0("bv"), g0("bo"),
                   g0("norm_w"), g0("norm_b")),
        pack_layer(np, g1("wq").T, g1("wk").T, g1("bq"), g1("bk"), g1("wv"), g1("wo").T, g1("bv"), g1("bo"),
                   g1("gamma"), g1("beta")),
    ])
    per_group = C // 32
    group = np.arange(P) % C // per_group
    consts = np.concatenate([np.eye(P), (group[:, None] == group[None, :]) / (4 * per_group)], 1).astype(np.float32)

    nc = bacc.Bacc("TRN2", target_bir_lowering=False, num_devices=1)
    arrays = {"x_dram": xh, "layers_dram": layers, "consts_dram": consts}
    aps = [nc.dram_tensor(k, v.shape, F32, kind="ExternalInput").ap() for k, v in arrays.items()]
    out = nc.dram_tensor("out_dram", xh.shape, F32, kind="ExternalOutput").ap()
    attention_pair(nc, *aps, out)
    r = run_bass_kernel_spmd(nc, [arrays], core_ids=[0])
    got = r.results[0]["out_dram"]
    return got.reshape(B, 2, C, half).transpose(0, 2, 1, 3).reshape(B, C, H, W)
```
